# Optimizing a Trainium2 kernel written in Bass

```python
import numpy as np
import jax
import jax.numpy as jnp

def _softmax(x, axis=-1):
    return jax.nn.softmax(x, axis=axis)

def _gelu(x):
    return jax.nn.gelu(x, approximate=True)

def _silu(x):
    return jax.nn.silu(x)

def _sigmoid(x):
    return jax.nn.sigmoid(x)

def _layernorm(x, axis=-1, eps=1e-05):
    m = jnp.mean(x, axis=axis, keepdims=True)
    v = jnp.var(x, axis=axis, keepdims=True)
    return (x - m) / jnp.sqrt(v + eps)

def _scatter_add(tgt, idx, src, axis=0):
    return tgt.at[idx].add(src)

def _segment_sum(src, seg, n):
    return jax.ops.segment_sum(src, seg, n)
kernel_name = 'mk_recurrent_d1_jaxref_r8_b316b1'

def setup_inputs(seed: int=0):
    np.random.seed(seed)
    _w = jnp.asarray

    def _L0_attn_setup():
        import jax, jax.numpy as jnp
        import numpy as np
        from jax import lax
        D_MODEL = 256
        D_STATE = 64
        D_CONV = 4
        EXPAND = 2
        HEADDIM = 128
        NGROUPS = 1
        CHUNK = 32
        D_INNER = EXPAND * D_MODEL
        NHEADS = D_INNER // HEADDIM
        D_IN_PROJ = 2 * D_INNER + 2 * NGROUPS * D_STATE + NHEADS
        CONV_DIM = D_INNER + 2 * NGROUPS * D_STATE
        EPS = 1e-05

        def segsum(x):
            T = x.shape[-1]
            xr = jnp.broadcast_to(x[..., :, None], x.shape + (T,))
            mask_lo = jnp.tril(jnp.ones((T, T), bool), -1)
            xr = jnp.where(mask_lo, xr, 0.0)
            seg = jnp.cumsum(xr, axis=-2)
            mask = jnp.tril(jnp.ones((T, T), bool), 0)
            return jnp.where(mask, seg, -jnp.inf)

        def ssd_minimal_discrete(X, A, B, C, block_len):
            b, L, h, p = X.shape
            n = B.shape[-1]
            c = L // block_len
            X = X.reshape(b, c, block_len, h, p)
            B = B.reshape(b, c, block_len, h, n)
            C = C.reshape(b, c, block_len, h, n)
            A = A.reshape(b, c, block_len, h).transpose(0, 3, 1, 2)
            A_cumsum = jnp.cumsum(A, axis=-1)
            Lmat = jnp.exp(segsum(A))
            Y_diag = jnp.einsum('bclhn,bcshn,bhcls,bcshp->bclhp', C, B, Lmat, X)
            decay_states = jnp.exp(A_cumsum[:, :, :, -1:] - A_cumsum)
            states = jnp.einsum('bclhn,bhcl,bclhp->bchpn', B, decay_states, X)
            init = jnp.zeros_like(states[:, :1])
            states = jnp.concatenate([init, states], axis=1)
            A_last = jnp.pad(A_cumsum[:, :, :, -1], ((0, 0), (0, 0), (1, 0)))
            decay_chunk = jnp.exp(segsum(A_last))
            new_states = jnp.einsum('bhzc,bchpn->bzhpn', decay_chunk, states)
            states, final_state = (new_states[:, :-1], new_states[:, -1])
            state_decay_out = jnp.exp(A_cumsum)
            Y_off = jnp.einsum('bclhn,bchpn,bhcl->bclhp', C, states, state_decay_out)
            Y = (Y_diag + Y_off).reshape(b, L, h, p)
            return (Y, final_state)
        key = jax.random.key(seed)
        ks = jax.random.split(key, 6)
        Bsz, Lsz = (2, 256)
        return {'u': jax.random.normal(ks[0], (Bsz, Lsz, D_MODEL), jnp.float32), 'W_in': jax.random.normal(ks[1], (D_IN_PROJ, D_MODEL), jnp.float32) * 0.02, 'W_conv': jax.random.normal(ks[2], (CONV_DIM, 1, D_CONV), jnp.float32) * 0.2, 'b_conv': jnp.zeros((CONV_DIM,), jnp.float32), 'dt_bias': jax.random.normal(ks[3], (NHEADS,), jnp.float32) * 0.5, 'A_log': jax.random.uniform(ks[4], (NHEADS,), jnp.float32, 0.0, 2.77), 'D': jnp.ones((NHEADS,), jnp.float32), 'norm_w': jnp.ones((D_INNER,), jnp.float32), 'W_out': jax.random.normal(ks[5], (D_MODEL, D_INNER), jnp.float32) * 0.02}
    _L0_attn_in = _L0_attn_setup()

    def _L0_ffn_setup():
        import jax, jax.numpy as jnp
        import numpy as np
        D_MODEL = 256
        HIDDEN = 4 * D_MODEL
        N_EXPERTS = 8
        TOP_K = 2
        CAP_FACTOR = 1.0
        key = jax.random.key(seed)
        ks = jax.random.split(key, 6)
        x = jax.random.normal(ks[0], (4, 256, D_MODEL), dtype=jnp.float32)
        wg = jax.random.normal(ks[1], (D_MODEL, N_EXPERTS), dtype=jnp.float32) * (1.0 / np.sqrt(D_MODEL))
        fc1_w = jax.random.normal(ks[2], (N_EXPERTS, D_MODEL, HIDDEN), dtype=jnp.float32) * 0.02
        fc1_b = jnp.zeros((N_EXPERTS, HIDDEN), dtype=jnp.float32)
        fc2_w = jax.random.normal(ks[3], (N_EXPERTS, HIDDEN, D_MODEL), dtype=jnp.float32) * 0.02
        fc2_b = jnp.zeros((N_EXPERTS, D_MODEL), dtype=jnp.float32)
        return {'x': x, 'wg': wg, 'fc1_w': fc1_w, 'fc1_b': fc1_b, 'fc2_w': fc2_w, 'fc2_b': fc2_b}
    _L0_ffn_in = _L0_ffn_setup()
    _d = {'L0_attn_u': _L0_attn_in['u'], 'L0_attn_W_in': _L0_attn_in['W_in'], 'L0_attn_W_conv': _L0_attn_in['W_conv'], 'L0_attn_b_conv': _L0_attn_in['b_conv'], 'L0_attn_dt_bias': _L0_attn_in['dt_bias'], 'L0_attn_A_log': _L0_attn_in['A_log'], 'L0_attn_D': _L0_attn_in['D'], 'L0_attn_norm_w': _L0_attn_in['norm_w'], 'L0_attn_W_out': _L0_attn_in['W_out'], 'L0_ffn_wg': _L0_ffn_in['wg'], 'L0_ffn_fc1_w': _L0_ffn_in['fc1_w'], 'L0_ffn_fc1_b': _L0_ffn_in['fc1_b'], 'L0_ffn_fc2_w': _L0_ffn_in['fc2_w'], 'L0_ffn_fc2_b': _L0_ffn_in['fc2_b']}
    _x0 = _d['L0_attn_u']
    _d['L0_attn_u'] = jax.random.normal(jax.random.fold_in(jax.random.key(seed), 1), (4, 256, 256), dtype=_x0.dtype)
    del _x0
    return _d

def reference(L0_attn_u, L0_attn_W_in, L0_attn_W_conv, L0_attn_b_conv, L0_attn_dt_bias, L0_attn_A_log, L0_attn_D, L0_attn_norm_w, L0_attn_W_out, L0_ffn_wg, L0_ffn_fc1_w, L0_ffn_fc1_b, L0_ffn_fc2_w, L0_ffn_fc2_b):

    def _L0_attn_ref(u, W_in, W_conv, b_conv, dt_bias, A_log, D, norm_w, W_out):
        import jax, jax.numpy as jnp
        import numpy as np
        from jax import lax
        D_MODEL = 256
        D_STATE = 64
        D_CONV = 4
        EXPAND = 2
        HEADDIM = 128
        NGROUPS = 1
        CHUNK = 32
        D_INNER = EXPAND * D_MODEL
        NHEADS = D_INNER // HEADDIM
        D_IN_PROJ = 2 * D_INNER + 2 * NGROUPS * D_STATE + NHEADS
        CONV_DIM = D_INNER + 2 * NGROUPS * D_STATE
        EPS = 1e-05

        def segsum(x):
            T = x.shape[-1]
            xr = jnp.broadcast_to(x[..., :, None], x.shape + (T,))
            mask_lo = jnp.tril(jnp.ones((T, T), bool), -1)
            xr = jnp.where(mask_lo, xr, 0.0)
            seg = jnp.cumsum(xr, axis=-2)
            mask = jnp.tril(jnp.ones((T, T), bool), 0)
            return jnp.where(mask, seg, -jnp.inf)

        def ssd_minimal_discrete(X, A, B, C, block_len):
            b, L, h, p = X.shape
            n = B.shape[-1]
            c = L // block_len
            X = X.reshape(b, c, block_len, h, p)
            B = B.reshape(b, c, block_len, h, n)
            C = C.reshape(b, c, block_len, h, n)
            A = A.reshape(b, c, block_len, h).transpose(0, 3, 1, 2)
            A_cumsum = jnp.cumsum(A, axis=-1)
            Lmat = jnp.exp(segsum(A))
            Y_diag = jnp.einsum('bclhn,bcshn,bhcls,bcshp->bclhp', C, B, Lmat, X)
            decay_states = jnp.exp(A_cumsum[:, :, :, -1:] - A_cumsum)
            states = jnp.einsum('bclhn,bhcl,bclhp->bchpn', B, decay_states, X)
            init = jnp.zeros_like(states[:, :1])
            states = jnp.concatenate([init, states], axis=1)
            A_last = jnp.pad(A_cumsum[:, :, :, -1], ((0, 0), (0, 0), (1, 0)))
            decay_chunk = jnp.exp(segsum(A_last))
            new_states = jnp.einsum('bhzc,bchpn->bzhpn', decay_chunk, states)
            states, final_state = (new_states[:, :-1], new_states[:, -1])
            state_decay_out = jnp.exp(A_cumsum)
            Y_off = jnp.einsum('bclhn,bchpn,bhcl->bclhp', C, states, state_decay_out)
            Y = (Y_diag + Y_off).reshape(b, L, h, p)
            return (Y, final_state)
        b, L, _ = u.shape
        zxbcdt = u @ W_in.T
        z = zxbcdt[..., :D_INNER]
        xBC = zxbcdt[..., D_INNER:D_INNER + CONV_DIM]
        dt = zxbcdt[..., D_INNER + CONV_DIM:]
        dt = jax.nn.softplus(dt + dt_bias)
        xc = lax.conv_general_dilated(xBC.transpose(0, 2, 1), W_conv, (1,), [(D_CONV - 1, 0)], dimension_numbers=('NCH', 'OIH', 'NCH'), feature_group_count=CONV_DIM)
        xBC = jax.nn.silu((xc + b_conv[None, :, None]).transpose(0, 2, 1))
        x = xBC[..., :D_INNER].reshape(b, L, NHEADS, HEADDIM)
        Bm = xBC[..., D_INNER:D_INNER + NGROUPS * D_STATE]
        Cm = xBC[..., D_INNER + NGROUPS * D_STATE:]
        Bm = jnp.broadcast_to(Bm.reshape(b, L, NGROUPS, D_STATE), (b, L, NHEADS, D_STATE))
        Cm = jnp.broadcast_to(Cm.reshape(b, L, NGROUPS, D_STATE), (b, L, NHEADS, D_STATE))
        A = -jnp.exp(A_log)
        x_scaled = x * dt[..., None]
        A_dt = A[None, None, :] * dt
        Y, _final = ssd_minimal_discrete(x_scaled, A_dt, Bm, Cm, CHUNK)
        y = Y + x * D[None, None, :, None]
        y = y.reshape(b, L, D_INNER)
        g = y * jax.nn.silu(z)
        y = g * lax.rsqrt(jnp.mean(g * g, axis=-1, keepdims=True) + EPS) * norm_w
        return y @ W_out.T

    def _L0_ffn_ref(x, wg, fc1_w, fc1_b, fc2_w, fc2_b):
        import jax, jax.numpy as jnp
        import numpy as np
        D_MODEL = 256
        HIDDEN = 4 * D_MODEL
        N_EXPERTS = 8
        TOP_K = 2
        CAP_FACTOR = 1.0
        B, L, D = x.shape
        S = B * L
        E = wg.shape[1]
        K = TOP_K
        C = int(K * S * CAP_FACTOR) // E
        xt = x.reshape(S, D)
        scores = jax.nn.softmax(xt.astype(jnp.float32) @ wg.astype(jnp.float32), axis=-1)
        gate_vals, idx = jax.lax.top_k(scores, K)
        gate_vals = gate_vals / jnp.clip(jnp.sum(gate_vals, axis=-1, keepdims=True), 1e-09)
        counts = jnp.zeros((E,), jnp.int32)
        disp = jnp.zeros((E, C, D), x.dtype)
        pos_safe_l, valid_l = ([], [])
        for s in range(K):
            mask = jax.nn.one_hot(idx[:, s], E, dtype=jnp.int32)
            loc = jnp.cumsum(mask, axis=0) - 1 + counts[None, :]
            pos = jnp.sum(loc * mask, axis=-1)
            counts = counts + jnp.sum(mask, axis=0)
            valid = pos < C
            pos_safe = jnp.where(valid, pos, 0)
            disp = disp.at[idx[:, s], pos_safe].add(xt * valid[:, None].astype(x.dtype))
            pos_safe_l.append(pos_safe)
            valid_l.append(valid)
        h = jax.nn.gelu(jnp.einsum('ecd,edh->ech', disp, fc1_w) + fc1_b[:, None, :], approximate=False)
        eo = jnp.einsum('ech,ehd->ecd', h, fc2_w) + fc2_b[:, None, :]
        y = jnp.zeros((S, D), x.dtype)
        for s in range(K):
            g = (gate_vals[:, s] * valid_l[s].astype(gate_vals.dtype)).astype(x.dtype)
            y = y + g[:, None] * eo[idx[:, s], pos_safe_l[s]]
        return y.reshape(B, L, D)
    x = L0_attn_u
    xn = _layernorm(x, axis=-1)
    s = _L0_attn_ref(xn, L0_attn_W_in, L0_attn_W_conv, L0_attn_b_conv, L0_attn_dt_bias, L0_attn_A_log, L0_attn_D, L0_attn_norm_w, L0_attn_W_out)
    g = _silu(_L0_ffn_ref(xn, L0_ffn_wg, L0_ffn_fc1_w, L0_ffn_fc1_b, L0_ffn_fc2_w, L0_ffn_fc2_b))
    x = x + s * g
    return x

_drawn_inputs = setup_inputs


def setup_inputs(seed=0):
    import zlib

    import numpy as np

    out = dict(_drawn_inputs(seed))
    spreads = {'L0_attn_b_conv': (0.0, 0.482),
     'L0_attn_D': (1.0, 0.6),
     'L0_attn_norm_w': (1.0, 0.6),
     'L0_ffn_fc1_b': (0.0, 0.8),
     'L0_ffn_fc2_b': (0.0, 0.481)}
    factors = {'L0_attn_W_conv': 2.725,
     'L0_attn_dt_bias': 8.0,
     'L0_attn_A_log': 8.0,
     'L0_ffn_fc1_w': 3.104,
     'L0_ffn_fc2_w': 2.887}
    for name, (base, spread) in spreads.items():
        noise = np.random.default_rng([zlib.crc32(name.encode()), seed]).standard_normal(out[name].shape)
        drawn = base * np.exp(spread * noise) if base else spread * noise
        out[name] = jnp.asarray(drawn.astype(out[name].dtype))
    for name, factor in factors.items():
        out[name] = (out[name] * factor).astype(out[name].dtype)
    return out
```

```python
from contextlib import ExitStack

import concourse.bass as bass
from concourse import mybir

F32 = mybir.dt.float32
BF16 = mybir.dt.bfloat16
I32 = mybir.dt.int32
U32 = mybir.dt.uint32
ALU = mybir.AluOpType
ACT = mybir.ActivationFunctionType
AX_X = mybir.AxisListType.X

P = 128
TAPS = 4
EPS = 1e-5
DROPPED = float(1 << 20)


def layer(nc, x, w_in_t, w_small, head_params, channel_params, w_out_t,
          fc1_w, fc1_b, fc2_w, fc2_b, out):
    TOKENS, DM = x.shape
    KD = DM // P
    TILES = TOKENS // P
    HEADS = head_params.shape[1] // 3
    DI = w_out_t.shape[0]
    HT = DI // P
    STATE = (w_in_t.shape[1] - 2 * DI - HEADS) // 2
    EXPERTS, _, HIDDEN = fc1_w.shape
    FT = HIDDEN // P
    CHOICES = 2
    CAP = CHOICES * TOKENS // EXPERTS
    SLOTS = EXPERTS * CAP
    CH = CAP // P
    REC = DM + 2
    SPAN = 512
    SPANS = TOKENS // SPAN
    TPS = SPAN // P
    SEQ = 256
    NSMALL = HEADS + EXPERTS
    CTILES = HT + 1
    assert HT == HEADS and STATE == 64 and CH == 2 and KD == 2

    slots_dram = nc.dram_tensor("expert_slots", [SLOTS, REC], F32).ap()
    moe_dram = nc.dram_tensor("moe_rows", [CHOICES * TOKENS, DM], F32).ap()

    with ExitStack() as ctx:
        def sb(name, shape, dt=F32):
            return ctx.enter_context(nc.sbuf_tensor(name, shape, dt))

        def sem(name):
            return ctx.enter_context(nc.semaphore(name))

        bank = [ctx.enter_context(nc.psum_tensor(f"bank{i}", [P, 512], F32)) for i in range(8)]

        x_sb = sb("x_sb", [P, TILES, DM])
        rec = sb("rec", [P, CHOICES, TILES, REC])
        xn_t = sb("xn_t", [P, KD, TOKENS])
        win = sb("win", [P, KD, w_in_t.shape[1]])
        wsmall = sb("wsmall", [P, KD, NSMALL])
        heads = sb("heads", [P, 3 * HEADS])
        chan = sb("chan", [P, CTILES * TAPS + CTILES + HT])
        wout = sb("wout", [P, HT, DM])
        zs = sb("zs", [P, HT, TOKENS])
        xc = sb("xc", [P, HT, TOKENS])
        bc = sb("bc", [P, TOKENS])
        c_low = sb("c_low", [STATE, TOKENS])
        conv = sb("conv", [P, 2, SPAN])
        ident = sb("ident", [P, P])
        later = sb("later", [P, P])
        upto = sb("upto", [P, P])
        ones = sb("ones", [P, STATE])
        before16 = sb("before16", [P, P], BF16)
        ones16 = sb("ones16", [P, P], BF16)
        zeros = sb("zeros", [P, 4 * REC])
        prefer = sb("prefer", [P, EXPERTS])
        slot0 = sb("slot0", [P, CHOICES * TILES, EXPERTS])
        bn = sb("bn", [P, TILES, 6])
        mv = sb("mv", [P, TILES, 2])
        std = sb("std", [P, TILES])
        rstd = sb("rstd", [P, TILES])
        lg = sb("lg", [P, TILES, EXPERTS])
        ex = sb("ex", [P, TILES, EXPERTS])
        sc = sb("sc", [P, CHOICES, TILES, EXPERTS])
        key = sb("key", [P, TILES, EXPERTS])
        stat = sb("stat", [P, 10, TILES])
        hot = sb("hot", [P, CHOICES * TILES, EXPERTS], BF16)
        place = sb("place", [P, 3, CHOICES * TILES, EXPERTS])
        slot_f = sb("slot_f", [P, CHOICES * TILES])
        slot_i = sb("slot_i", [P, CHOICES * TILES], I32)
        dtw = sb("dtw", [P, 10, TILES, HEADS])
        a_exp = sb("a_exp", [P, HEADS])
        a_dt = sb("a_dt", [P, TILES, HEADS])
        dt_sb = sb("dt_sb", [P, TILES, HEADS])
        decay = sb("decay", [P, TILES, HEADS])
        steps = sb("steps", [P, 2, HEADS, P])
        seg = sb("seg", [P, 2, HEADS, P])
        cb = sb("cb", [P, 2, P])
        xs = sb("xs", [P, 2, HEADS, P])
        xd = sb("xd", [P, HEADS, P])
        b_tok = sb("b_tok", [P, STATE])
        state = sb("state", [STATE, HEADS, P])
        c_dec = sb("c_dec", [STATE, HEADS, P])
        g = sb("g", [P, 2, HT, P])
        gsq = sb("gsq", [P, 2, HT, P])
        s_out = sb("s_out", [P, TILES, DM])
        rms = sb("rms", [P, 4, TILES])
        w1 = sb("w1", [P, 2, KD, HIDDEN])
        w2 = sb("w2", [P, 2, FT, DM])
        b1 = sb("b1", [P, 2, FT])
        b2 = sb("b2", [P, 2, DM])
        slots = sb("slots", [P, 2, CH, REC])
        slots_t = sb("slots_t", [P, 2, KD, CAP])
        hid = sb("hid", [P, FT, CAP])
        eo = sb("eo", [P, 2, CH, DM])
        row_t = sb("row_t", [P, 2, CH])
        row_i = sb("row_i", [P, 2, CH], I32)
        moe = zs[:, :, :].rearrange("p a (t c) -> p (a t) c", c=DM)
        moe = moe.rearrange("p (k t) c -> p k t c", k=CHOICES)

        x_loaded = [sem(f"x_loaded{i}") for i in range(2)]
        small_loaded = sem("small_loaded")
        win_loaded = [sem(f"win_loaded{i}") for i in range(2)]
        wout_loaded = sem("wout_loaded")
        zeros_ready = sem("zeros_ready")
        dram_cleared = sem("dram_cleared")
        masks_ready = sem("masks_ready")
        pool_steps = sem("pool_steps")
        dve_steps = sem("dve_steps")
        var_ready = sem("var_ready")
        std_ready = sem("std_ready")
        xn_ready = sem("xn_ready")
        rec_copied = sem("rec_copied")
        xn_t_psum = sem("xn_t_psum")
        xn_t_ready = sem("xn_t_ready")
        small_psum = sem("small_psum")
        exp_in_ready = sem("exp_in_ready")
        exp_out_ready = sem("exp_out_ready")
        hot_ready = sem("hot_ready")
        place_psum = sem("place_psum")
        slots_known = sem("slots_known")
        gates_ready = sem("gates_ready")
        scattered = [sem(f"scattered{i}") for i in range(4)]
        proj_psum = sem("proj_psum")
        proj_read = sem("proj_read")
        tap_ready = sem("tap_ready")
        conv_ready = sem("conv_ready")
        conv_read = sem("conv_read")
        z_ready = sem("z_ready")
        c_moved = [sem(f"c_moved{i}") for i in range(SPANS)]
        a_dt_ready = sem("a_dt_ready")
        decay_psum = sem("decay_psum")
        decay_ready = sem("decay_ready")
        steps_ready = sem("steps_ready")
        wout_scaled = sem("wout_scaled")
        xt_psum = sem("xt_psum")
        xs_ready = sem("xs_ready")
        seg_psum = sem("seg_psum")
        seg_ready = sem("seg_ready")
        cb_psum = sem("cb_psum")
        cb_ready = sem("cb_ready")
        mix_ready = sem("mix_ready")
        b_tok_psum = sem("b_tok_psum")
        b_tok_ready = sem("b_tok_ready")
        cdec_psum = sem("cdec_psum")
        cexp_ready = sem("cexp_ready")
        cdec_ready = sem("cdec_ready")
        state_psum = sem("state_psum")
        state_ready = sem("state_ready")
        y_psum = sem("y_psum")
        g_ready = sem("g_ready")
        gsq_ready = sem("gsq_ready")
        s_psum = sem("s_psum")
        s_ready = sem("s_ready")
        w_loaded = [[sem(f"w{j}_loaded{u}") for u in range(2)] for j in (1, 2)]
        bias_loaded = [sem(f"bias_loaded{u}") for u in range(2)]
        slots_loaded = [sem(f"slots_loaded{u}") for u in range(2)]
        slots_t_psum = sem("slots_t_psum")
        slots_t_ready = sem("slots_t_ready")
        fc1_psum = sem("fc1_psum")
        hid_ready = sem("hid_ready")
        fc2_psum = sem("fc2_psum")
        fc2_read = sem("fc2_read")
        rows_step = sem("rows_step")
        xd_ready = sem("xd_ready")
        y_read = sem("y_read")
        eo_ready = sem("eo_ready")
        eo_free = sem("eo_free")
        rows_scattered = [[sem(f"rows_scattered{u}{h}") for h in range(CH)] for u in range(2)]
        moe_loaded = [[sem(f"moe_loaded{k}{i}") for i in range(4)] for k in range(CHOICES)]
        moe_summed = sem("moe_summed")
        moe_silu = sem("moe_silu")
        out_ready = sem("out_ready")
        stored = sem("stored")

        x_v = x.rearrange("(t p) d -> p t d", p=P)
        out_v = out.rearrange("(t p) d -> p t d", p=P)
        moe_v = moe_dram.rearrange("(k t p) d -> p k t d", p=P, k=CHOICES)
        slots_v = slots_dram.rearrange("(e h p) r -> e p h r", p=P, h=CH)
        win_v = w_in_t.rearrange("(k p) c -> p k c", p=P)
        w1_v = fc1_w.rearrange("e (k p) f -> e p k f", p=P)
        w2_v = fc2_w.rearrange("e (f p) d -> e p f d", p=P)
        HALF = TILES // 2
        EPI = 2
        LAST = EXPERTS // EPI - 1

        dt_bias = heads[:, 0:HEADS]
        a_log = heads[:, HEADS:2 * HEADS]

        def d_skip(h):
            return heads[:, 2 * HEADS + h:2 * HEADS + h + 1]

        def tap(c, j):
            return chan[:, c * TAPS + j:c * TAPS + j + 1]

        def conv_bias(c):
            return chan[:, CTILES * TAPS + c:CTILES * TAPS + c + 1]

        def norm_w(h):
            return chan[:, CTILES * TAPS + CTILES + h:CTILES * TAPS + CTILES + h + 1]

        PROJ = [("z", m, n) for m in range(HT) for n in range(SPANS)]
        PROJ += [("xbc", m, n) for n in range(SPANS) for m in [HT] + list(range(HT))]
        PROJ_BANKS = [4, 5, 6, 7]
        FC1_BANKS = [1, 2, 3]
        FC2_BANKS = [4, 5]
        NB1 = len(FC1_BANKS)
        XBC = [(i, m, n) for i, (kind, m, n) in enumerate(PROJ) if kind == "xbc"]

        def col0(kind, m):
            return m * P if kind == "z" else DI + m * P

        def convolved(c, n):
            return next(j for j, (_, m, nn) in enumerate(XBC) if (m, nn) == (c, n)) + 1

        block = ctx.enter_context(nc.Block())

        @block.sync
        def _(sp):
            for i in range(2):
                half = slice(i * HALF, (i + 1) * HALF)
                sp.dma_start(x_sb[:, half, :], x_v[:, half, :]).then_inc(x_loaded[i], 16)
            for n in range(2):
                c = slice(n * DI, DI if n == 0 else w_in_t.shape[1])
                sp.dma_start(win[:, :, c], win_v[:, :, c]).then_inc(win_loaded[n], 16)
            sp.wait_ge(zeros_ready, 1)
            for i in range(SLOTS // (4 * P)):
                dst = slots_dram[i * 4 * P:(i + 1) * 4 * P, :].rearrange("(p r) c -> p (r c)", p=P)
                sp.dma_start(dst, zeros[:, :]).then_inc(dram_cleared, 16)
            for i in range(CHOICES * TOKENS // (4 * P)):
                dst = moe_dram[i * 4 * P:(i + 1) * 4 * P, :].rearrange("(p r) c -> p (r c)", p=P)
                sp.dma_start(dst, zeros[:, 0:4 * DM]).then_inc(dram_cleared, 16)
            sp.dma_start(wout[:, :, :], w_out_t.rearrange("(h p) d -> p h d", p=P)).then_inc(wout_loaded, 16)

            def load_weights(e, u):
                sp.dma_start(w1[:, u, :, :], w1_v[bass.ds(e, 1)].rearrange("e p k f -> (e p) k f")
                             ).then_inc(w_loaded[0][u], 16)
                sp.dma_start(w2[:, u, :, :], w2_v[bass.ds(e, 1)].rearrange("e p f d -> (e p) f d")
                             ).then_inc(w_loaded[1][u], 16)
                sp.dma_start(b1[:, u, :], fc1_b[bass.ds(e, 1)].rearrange("e p f -> (e p) f")
                             ).then_inc(bias_loaded[u], 16)
                sp.dma_start(b2[:, u, :], fc2_b[bass.ds(e, 1)].to_broadcast([P, DM])
                             ).then_inc(bias_loaded[u], 16)

            def load_slots(e, u):
                sp.dma_start(slots[:, u, :, :], slots_v[bass.ds(e, 1)].rearrange("e p h r -> (e p) h r")
                             ).then_inc(slots_loaded[u], 16)

            load_weights(0, 0)
            for n in range(SPANS):
                sp.wait_ge(conv_read, convolved(HT, n))
                span = slice(n * SPAN, (n + 1) * SPAN)
                sp.dma_start(c_low[:, span], bc[STATE:2 * STATE, span]).then_inc(c_moved[n], 16)
                if n == 0:
                    load_weights(1, 1)
            for s in scattered:
                sp.wait_ge(s, 16 * CHOICES * TILES // 4)
            load_slots(0, 0)
            load_slots(1, 1)

            def refill(e, u):
                sp.wait_ge(fc2_psum, (e - 1) * CH)
                sp.wait_ge(eo_ready, (e - 1) * CH)
                load_weights(e, u)
                load_slots(e, u)

            with sp.Fori(1, LAST) as i:
                for u in range(EPI):
                    refill(i * EPI + u, u)
            for u in range(EPI):
                refill(LAST * EPI + u, u)

            for u in range(EPI):
                for h in range(CH):
                    sp.wait_ge(rows_scattered[u][h], 16 * (LAST + 1))
            for i in range(4):
                t = slice(2 * i, 2 * i + 2)
                sp.dma_start(moe[:, 0, t, :], moe_v[:, 0, t, :]).then_inc(moe_loaded[0][i], 16)
            for i in range(4):
                t = slice(2 * i, 2 * i + 2)
                sp.wait_ge(out_ready, i + 1)
                sp.dma_start(out_v[:, t, :], s_out[:, t, :]).then_inc(stored, 16)
            sp.wait_ge(stored, 16 * 4)

        @block.gpsimd
        def _(pool):
            done = [0]

            def step(ins):
                done[0] += 1
                return ins.then_inc(pool_steps, 1)

            nc.gpsimd.memset(zeros[:, :], 0.0).then_inc(zeros_ready, 1)
            step(nc.gpsimd.memset(ident[:, :], 0.0))
            step(nc.gpsimd.memset(later[:, :], 1.0))
            step(nc.gpsimd.memset(upto[:, :], 1.0))
            step(nc.gpsimd.memset(before16[:, :], 1.0))
            pool.wait_ge(pool_steps, 4)
            nc.gpsimd.affine_select(out=ident[:, :], in_=ident[:, :], compare_op=ALU.not_equal, fill=1.0,
                                    base=0, pattern=[[-1, P]], channel_multiplier=1).then_inc(masks_ready, 1)
            nc.gpsimd.affine_select(out=before16[:, :], in_=before16[:, :], compare_op=ALU.is_gt, fill=0.0,
                                    base=0, pattern=[[1, P]], channel_multiplier=-1).then_inc(masks_ready, 1)
            nc.gpsimd.memset(ones16[:, :], 1.0).then_inc(masks_ready, 1)
            nc.gpsimd.iota(prefer[:, :], pattern=[[-1, EXPERTS]], base=EXPERTS, channel_multiplier=0,
                           allow_small_or_imprecise_dtypes=True).then_inc(masks_ready, 1)
            nc.gpsimd.iota(slot0[:, :, :], pattern=[[0, CHOICES * TILES], [CAP, EXPERTS]], base=0,
                           channel_multiplier=0, allow_small_or_imprecise_dtypes=True).then_inc(masks_ready, 1)
            nc.gpsimd.affine_select(out=later[:, :], in_=later[:, :], compare_op=ALU.is_gt, fill=0.0,
                                    base=0, pattern=[[-1, P]], channel_multiplier=1).then_inc(masks_ready, 1)
            nc.gpsimd.affine_select(out=upto[:, :], in_=upto[:, :], compare_op=ALU.is_ge, fill=0.0,
                                    base=0, pattern=[[1, P]], channel_multiplier=-1).then_inc(masks_ready, 1)
            nc.gpsimd.memset(ones[:, :], 1.0).then_inc(masks_ready, 1)
            for k in range(CHOICES):
                nc.gpsimd.iota(rec[:, k, :, DM + 1], pattern=[[P, TILES]], base=k * TOKENS + 1,
                               channel_multiplier=1, allow_small_or_imprecise_dtypes=True
                               ).then_inc(rec_copied, 1)
            for t in range(TILES):
                pool.wait_ge(xn_ready, t + 1)
                nc.gpsimd.tensor_copy(rec[:, 1, t, 0:DM], rec[:, 0, t, 0:DM]).then_inc(rec_copied, 1)
            pool.wait_ge(rec_copied, CHOICES + TILES)
            pool.wait_ge(gates_ready, CHOICES)
            pool.wait_ge(slots_known, 1)
            pool.wait_ge(dram_cleared, 16 * (SLOTS + CHOICES * TOKENS) // (4 * P))
            for q in range(CHOICES * TILES):
                k, t = divmod(q, TILES)
                nc.gpsimd.indirect_dma_start(
                    out=slots_dram, out_offset=bass.IndirectOffsetOnAxis(ap=slot_i[:, q:q + 1].bitcast(U32), axis=0),
                    in_=rec[:, k, t, :], in_offset=None, bounds_check=SLOTS - 1, oob_is_err=False,
                ).then_inc(scattered[q % 4], 16)

            pool.wait_ge(a_dt_ready, 1)
            for c in range(TILES):
                if c >= 2:
                    pool.wait_ge(seg_psum, c - 1)
                if c >= 3:
                    pool.wait_ge(cdec_psum, (c - 1) // 2)
                nc.gpsimd.tensor_tensor(
                    steps[:, c % 2, :, :], a_dt[:, c, :].unsqueeze(2).to_broadcast([P, HEADS, P]),
                    upto[:, :].unsqueeze(1).to_broadcast([P, HEADS, P]), ALU.mult).then_inc(steps_ready, 1)

            def scatter_rows(e, u):
                for h in range(CH):
                    pool.wait_ge(eo_ready, e * CH + h + 1)
                    nc.gpsimd.indirect_dma_start(
                        out=moe_dram,
                        out_offset=bass.IndirectOffsetOnAxis(ap=row_i[:, u, h:h + 1].bitcast(U32), axis=0),
                        in_=eo[:, u, h, :], in_offset=None, bounds_check=CHOICES * TOKENS - 1,
                        oob_is_err=False).then_inc(rows_scattered[u][h], 16)
                for h in range(CH):
                    pool.wait_ge(rows_scattered[u][h], 16 * (e // EPI + 1))
                pool.sem_inc(eo_free, 1)

            pool.sem_inc(eo_free, EPI)
            for e in range(EXPERTS):
                scatter_rows(e, e % EPI)

        @block.scalar
        def _(act):
            act.dma_start(wsmall[:, :, :], w_small.rearrange("(k p) c -> p k c", p=P)).then_inc(small_loaded, 16)
            act.dma_start(heads[:, :], head_params[0:1, :].to_broadcast([P, 3 * HEADS])).then_inc(small_loaded, 16)
            act.dma_start(chan[:, :], channel_params).then_inc(small_loaded, 16)
            for i in range(2):
                half = slice(i * HALF, (i + 1) * HALF)
                act.wait_ge(var_ready, i + 1)
                nc.scalar.activation(std[:, half], stat[:, 9, half], ACT.Sqrt).then_inc(std_ready, 1)
            for t in range(TILES):
                act.wait_ge(xn_t_psum, t + 1)
                nc.scalar.copy(xn_t[:, :, t * P:(t + 1) * P],
                               bank[t % 2][:, 0:KD * P].rearrange("p (k c) -> p k c", k=KD)).then_inc(xn_t_ready, 1)
            act.wait_ge(small_loaded, 48)
            nc.scalar.activation(a_exp[:, :], a_log, ACT.Exp).then_inc(exp_out_ready, 1)
            act.wait_ge(exp_in_ready, 1)
            nc.scalar.activation(ex[:, :, :], lg[:, :, :], ACT.Exp).then_inc(exp_out_ready, 1)
            act.wait_ge(exp_in_ready, 2)
            nc.scalar.activation(dtw[:, 2, :, :], dtw[:, 1, :, :], ACT.Exp).then_inc(exp_out_ready, 1)

            def conv_silu(j):
                _, m, n = XBC[j]
                act.wait_ge(conv_ready, j + 1)
                dst = bc[:, n * SPAN:(n + 1) * SPAN] if m == HT else xc[:, m, n * SPAN:(n + 1) * SPAN]
                nc.scalar.activation(dst, conv[:, j % 2, :], ACT.Silu, bias=conv_bias(m)).then_inc(conv_read, 1)

            j = 0
            for i, (kind, m, n) in enumerate(PROJ):
                src = bank[PROJ_BANKS[i % 4]]
                if kind == "z":
                    act.wait_ge(proj_psum, i + 1)
                    nc.scalar.activation(zs[:, m, n * SPAN:(n + 1) * SPAN], src[:, :], ACT.Silu).then_inc(z_ready, 1)
                else:
                    if j >= 2:
                        conv_silu(j - 2)
                        act.wait_ge(conv_read, j - 1)
                    act.wait_ge(proj_psum, i + 1)
                    nc.scalar.activation(conv[:, j % 2, :], src[:, :], ACT.Copy, scale=tap(m, TAPS - 1)
                                         ).then_inc(tap_ready, 1)
                    j += 1
            conv_silu(j - 2)
            conv_silu(j - 1)

            act.wait_ge(decay_psum, 1)
            nc.scalar.activation(decay[:, :, :], bank[2][:, 0:TILES * HEADS].rearrange("p (t h) -> p t h", h=HEADS),
                                 ACT.Exp).then_inc(decay_ready, 1)

            def ssd_inputs(c):
                act.wait_ge(seg_psum, c + 1)
                if c >= 2:
                    act.wait_ge(y_psum, c - 1)
                nc.scalar.activation(seg[:, c % 2, :, :], bank[2][:, :].rearrange("p (h l) -> p h l", h=HEADS),
                                     ACT.Exp).then_inc(seg_ready, 1)
                if c % 2 == 0:
                    act.wait_ge(b_tok_psum, c // 2 + 1)
                    nc.scalar.copy(b_tok[:, :], bank[7][:, 0:STATE]).then_inc(b_tok_ready, 1)
                else:
                    act.wait_ge(cdec_psum, c // 2 + 1)
                    if c >= 3:
                        act.wait_ge(y_psum, c - 1)
                    nc.scalar.activation(c_dec[:, :, :], bank[4][0:STATE, :].rearrange("p (h l) -> p h l", h=HEADS),
                                         ACT.Exp).then_inc(cexp_ready, 1)

            def ssd_state(c):
                act.wait_ge(state_psum, c // 2 + 1)
                nc.scalar.copy(state[:, :, :], bank[7][0:STATE, :].rearrange("p (h l) -> p h l", h=HEADS)
                               ).then_inc(state_ready, 1)

            def ssd_outputs(c):
                act.wait_ge(g_ready, c + 1)
                if c >= 2:
                    act.wait_ge(s_psum, c - 1)
                nc.scalar.square(gsq[:, c % 2, :, :], g[:, c % 2, :, :]).then_inc(gsq_ready, 1)

            def ssd_store(c):
                act.wait_ge(s_psum, c + 1)
                last = nc.scalar.copy(s_out[:, c, :], bank[5][:, 0:DM])
                last.then_inc(s_ready, 1)

            ssd_inputs(0)
            for c in range(TILES):
                if c + 1 < TILES:
                    ssd_inputs(c + 1)
                if c % 2 == 0:
                    ssd_state(c)
                if c >= 1:
                    ssd_store(c - 1)
                ssd_outputs(c)
            ssd_store(TILES - 1)

            def gelus(e, i, u):
                act.wait_ge(bias_loaded[u], (i + 1) * 32)
                for f in range(FT):
                    act.wait_ge(fc1_psum, e * FT + f + 1)
                    nc.scalar.activation(hid[:, f, :], bank[FC1_BANKS[f % 3]][:, 0:CAP], ACT.Gelu,
                                         bias=b1[:, u, f:f + 1]).then_inc(hid_ready, 1)

            with act.Fori(0, LAST) as i:
                for u in range(EPI):
                    gelus(i * EPI + u, i, u)
            for u in range(EPI):
                gelus(LAST * EPI + u, LAST, u)

            for u in range(EPI):
                for h in range(CH):
                    act.wait_ge(rows_scattered[u][h], 16 * (LAST + 1))
            for i in range(4):
                t = slice(2 * i, 2 * i + 2)
                act.dma_start(moe[:, 1, t, :], moe_v[:, 1, t, :]).then_inc(moe_loaded[1][i], 16)
            for i in range(4):
                t = slice(2 * i, 2 * i + 2)
                act.wait_ge(moe_summed, i + 1)
                nc.scalar.activation(moe[:, 1, t, :], moe[:, 0, t, :], ACT.Silu).then_inc(moe_silu, 1)

        @block.vector
        def _(dve):
            chained = [0]

            def link(ins):
                chained[0] += 1
                ins.then_inc(dve_steps, 1)
                dve.wait_ge(dve_steps, chained[0])

            def step(ins):
                chained[0] += 1
                ins.then_inc(dve_steps, 1)

            V = nc.vector

            def stats(i):
                dve.wait_ge(x_loaded[i], 16)
                for t in range(i * HALF, (i + 1) * HALF):
                    step(V.bn_stats(bn[:, t, :], x_sb[:, t, :]))
                dve.wait_ge(dve_steps, chained[0])
                for t in range(i * HALF, (i + 1) * HALF):
                    step(V.bn_aggr(mv[:, t, :], bn[:, t, :]))
                dve.wait_ge(dve_steps, chained[0])
                half = slice(i * HALF, (i + 1) * HALF)
                V.tensor_scalar(stat[:, 9, half], mv[:, half, 1], EPS, None, ALU.add).then_inc(var_ready, 1)

            def normalise(i):
                half = slice(i * HALF, (i + 1) * HALF)
                dve.wait_ge(std_ready, i + 1)
                link(V.reciprocal(rstd[:, half], std[:, half]))
                for t in range(i * HALF, (i + 1) * HALF):
                    V.tensor_scalar(rec[:, 0, t, 0:DM], x_sb[:, t, :], mv[:, t, 0:1], rstd[:, t:t + 1],
                                    ALU.subtract, ALU.mult).then_inc(xn_ready, 1)

            stats(0)
            normalise(0)
            stats(1)
            normalise(1)

            def over_e(a):
                return a.unsqueeze(2).to_broadcast([P, a.shape[1], EXPERTS])

            small = bank[3][:, 0:TILES * NSMALL].rearrange("p (t c) -> p t c", c=NSMALL)
            logits = small[:, :, HEADS:NSMALL]
            dve.wait_ge(small_psum, 1)
            dve.wait_ge(small_loaded, 48)
            step(V.tensor_tensor(dtw[:, 0, :, :], small[:, :, 0:HEADS],
                                 dt_bias.unsqueeze(1).to_broadcast([P, TILES, HEADS]), ALU.add))
            link(V.tensor_reduce(stat[:, 0, :], logits, AX_X, ALU.max))
            V.tensor_tensor(lg[:, :, :], logits, over_e(stat[:, 0, :]), ALU.subtract).then_inc(exp_in_ready, 1)
            V.scalar_tensor_tensor(dtw[:, 1, :, :], dtw[:, 0, :, :], -1.0, dtw[:, 0, :, :],
                                   ALU.mult, ALU.min).then_inc(exp_in_ready, 1)
            dve.wait_ge(exp_out_ready, 2)
            link(V.tensor_reduce(stat[:, 1, :], ex[:, :, :], AX_X, ALU.add))
            link(V.reciprocal(stat[:, 2, :], stat[:, 1, :]))
            link(V.tensor_tensor(sc[:, 0, :, :], ex[:, :, :], over_e(stat[:, 2, :]), ALU.mult))
            dve.wait_ge(masks_ready, 8)
            for k in range(CHOICES):
                oh = hot[:, k * TILES:(k + 1) * TILES, :]
                link(V.tensor_reduce(stat[:, 3 + k, :], sc[:, k, :, :], AX_X, ALU.max))
                link(V.tensor_tensor(key[:, :, :], sc[:, k, :, :], over_e(stat[:, 3 + k, :]), ALU.is_equal))
                link(V.tensor_tensor(key[:, :, :], key[:, :, :],
                                     prefer[:, :].unsqueeze(1).to_broadcast([P, TILES, EXPERTS]), ALU.mult))
                link(V.tensor_reduce(stat[:, 5, :], key[:, :, :], AX_X, ALU.max))
                one_hot = V.tensor_tensor(oh, key[:, :, :], over_e(stat[:, 5, :]), ALU.is_equal)
                if k == 0:
                    link(one_hot)
                    link(V.scalar_tensor_tensor(sc[:, 1, :, :], oh, -2.0, sc[:, 0, :, :], ALU.mult, ALU.add))
            one_hot.then_inc(hot_ready, 1)
            link(V.tensor_tensor(stat[:, 6, :], stat[:, 3, :], stat[:, 4, :], ALU.add))
            link(V.tensor_scalar(stat[:, 6, :], stat[:, 6, :], 1e-9, None, ALU.max))
            link(V.reciprocal(stat[:, 7, :], stat[:, 6, :]))
            for k in range(CHOICES):
                V.tensor_tensor(rec[:, k, :, DM], stat[:, 3 + k, :], stat[:, 7, :], ALU.mult).then_inc(gates_ready, 1)

            dve.wait_ge(exp_out_ready, 3)
            e_, d_, z_, z2, p_ = (dtw[:, n, :, :] for n in (2, 3, 4, 5, 6))
            link(V.tensor_scalar(d_, e_, 2.0, None, ALU.add))
            link(V.reciprocal(d_, d_))
            link(V.tensor_tensor(z_, e_, d_, ALU.mult))
            link(V.tensor_tensor(z2, z_, z_, ALU.mult))
            link(V.tensor_scalar(p_, z2, 1.0 / 17, None, ALU.mult))
            for n in (15, 13, 11, 9, 7, 5, 3):
                link(V.scalar_tensor_tensor(p_, p_, 1.0 / n, z2, ALU.add, ALU.mult))
            step(V.tensor_scalar(dtw[:, 7, :, :], dtw[:, 0, :, :], 0.0, None, ALU.max))
            link(V.scalar_tensor_tensor(p_, p_, 1.0, z_, ALU.add, ALU.mult))
            link(V.scalar_tensor_tensor(dt_sb[:, :, :], p_, 2.0, dtw[:, 7, :, :], ALU.mult, ALU.add))
            V.scalar_tensor_tensor(a_dt[:, :, :], dt_sb[:, :, :], -1.0,
                                   a_exp[:, :].unsqueeze(1).to_broadcast([P, TILES, HEADS]),
                                   ALU.mult, ALU.mult).then_inc(a_dt_ready, 1)

            dve.wait_ge(place_psum, 1)
            places = bank[2][:, 0:P].rearrange("p (q e) -> p q e", e=EXPERTS)
            link(V.tensor_scalar(place[:, 0, :, :], places, float(CAP), DROPPED, ALU.is_ge, ALU.mult))
            link(V.tensor_tensor(place[:, 1, :, :], places, place[:, 0, :, :], ALU.add))
            link(V.tensor_tensor(place[:, 2, :, :], place[:, 1, :, :], slot0[:, :, :], ALU.add))
            link(V.tensor_tensor(place[:, 0, :, :], place[:, 2, :, :], hot[:, :, :], ALU.mult))
            link(V.tensor_reduce(slot_f[:, :], place[:, 0, :, :], AX_X, ALU.add))
            V.tensor_copy(slot_i[:, :], slot_f[:, :]).then_inc(slots_known, 1)

            for j, (i, m, n) in enumerate(XBC):
                src = bank[PROJ_BANKS[i % 4]][:, :].rearrange("p (b l) -> p b l", l=SEQ)
                acc = conv[:, j % 2, :].rearrange("p (b l) -> p b l", l=SEQ)
                dve.wait_ge(tap_ready, j + 1)
                for d in range(1, TAPS):
                    ins = V.scalar_tensor_tensor(acc[:, :, d:], src[:, :, 0:SEQ - d], tap(m, TAPS - 1 - d),
                                                 acc[:, :, d:], ALU.mult, ALU.add)
                    if d < TAPS - 1:
                        link(ins)
                ins.then_inc(conv_ready, 1)

            dve.wait_ge(wout_loaded, 16)
            for h in range(HT):
                V.tensor_scalar(wout[:, h, :], wout[:, h, :], norm_w(h), None, ALU.mult).then_inc(wout_scaled, 1)

            dve.wait_ge(decay_ready, 1)
            link(V.tensor_tensor(decay[:, :, :], decay[:, :, :], dt_sb[:, :, :], ALU.mult))
            dve.wait_ge(z_ready, HT * SPANS)

            def ssd_inputs(c):
                b = c % 2
                x_tok = bank[0][:, :].rearrange("p (h l) -> p h l", h=HEADS)
                dve.wait_ge(xt_psum, c + 1)
                if c >= 2:
                    dve.wait_ge(y_psum, c - 1)
                V.tensor_tensor(xs[:, b, :, :], x_tok, dt_sb[:, c, :].unsqueeze(2).to_broadcast([P, HEADS, P]),
                                ALU.mult).then_inc(xs_ready, 1)
                if b == 0:
                    if c >= 2:
                        dve.wait_ge(state_psum, c // 2)
                    V.tensor_tensor(xd[:, :, :], x_tok, decay[:, c, :].unsqueeze(2).to_broadcast([P, HEADS, P]),
                                    ALU.mult).then_inc(xd_ready, 1)
                dve.wait_ge(cb_psum, c + 1)
                V.tensor_tensor(cb[:, b, :], bank[1][:, 0:P], upto[:, :], ALU.mult).then_inc(cb_ready, 1)
                dve.wait_ge(cb_ready, c + 1)
                dve.wait_ge(seg_ready, c + 1)
                V.tensor_tensor(seg[:, b, :, :], seg[:, b, :, :], cb[:, b, :].unsqueeze(1).to_broadcast([P, HEADS, P]),
                                ALU.mult).then_inc(mix_ready, 1)
                if b == 1:
                    dve.wait_ge(c_moved[c // TPS], 16)
                    dve.wait_ge(cexp_ready, c // 2 + 1)
                    now = c_low[:, c * P:(c + 1) * P]
                    V.tensor_tensor(c_dec[:, :, :], c_dec[:, :, :],
                                    now.unsqueeze(1).to_broadcast([STATE, HEADS, P]), ALU.mult).then_inc(cdec_ready, 1)

            def ssd_outputs(c):
                dve.wait_ge(y_psum, c + 1)
                if c >= 2:
                    dve.wait_ge(s_psum, c - 1)
                now = slice(c * P, (c + 1) * P)
                for h in range(HT):
                    V.scalar_tensor_tensor(g[:, c % 2, h, :], xc[:, h, now], d_skip(h), bank[3][:, h * P:(h + 1) * P],
                                           ALU.mult, ALU.add).then_inc(y_read, 1)
                dve.wait_ge(y_read, HT * (c + 1))
                V.tensor_tensor(g[:, c % 2, :, :], g[:, c % 2, :, :], zs[:, :, now], ALU.mult).then_inc(g_ready, 1)

            ssd_inputs(0)
            for c in range(TILES):
                if c + 1 < TILES:
                    ssd_inputs(c + 1)
                ssd_outputs(c)

            def slots_to_sbuf(e, u):
                dve.wait_ge(slots_t_psum, e + 1)
                V.tensor_copy(slots_t[:, u, :, :], bank[0][:, :].rearrange("p (k s) -> p k s", k=KD)
                              ).then_inc(slots_t_ready, 1)

            def expert_rows(e, i, u, follow):
                if follow:
                    slots_to_sbuf(e + 1, 1 - u)
                dve.wait_ge(slots_loaded[u], (i + 1) * 16)
                dve.wait_ge(eo_free, e + 1)
                V.tensor_scalar(row_t[:, u, :], slots[:, u, :, DM + 1], 0.0, DROPPED, ALU.is_equal, ALU.mult
                                ).then_inc(rows_step, 1)
                dve.wait_ge(rows_step, e + 1)
                V.scalar_tensor_tensor(row_i[:, u, :], slots[:, u, :, DM + 1], -1.0, row_t[:, u, :],
                                       ALU.add, ALU.add)
                dve.wait_ge(bias_loaded[u], (i + 1) * 32)
                for h in range(CH):
                    dve.wait_ge(fc2_psum, e * CH + h + 1)
                    V.tensor_tensor(eo[:, u, h, :], bank[FC2_BANKS[h]][:, 0:DM], b2[:, u, :], ALU.add
                                    ).then_inc(fc2_read, 1)
                    dve.wait_ge(fc2_read, CH + e * CH + h + 1)
                    V.tensor_scalar(eo[:, u, h, :], eo[:, u, h, :], slots[:, u, h, DM:DM + 1], None, ALU.mult
                                    ).then_inc(eo_ready, 1)

            slots_to_sbuf(0, 0)

            dve.wait_ge(s_psum, TILES)
            ms, y_, t_ = rms[:, 0, :], rms[:, 1, :], rms[:, 2, :]
            link(V.tensor_scalar(ms, bank[6][:, 0:TILES], 1.0 / DI, EPS, ALU.mult, ALU.add))
            link(V.tensor_scalar(y_.bitcast(U32), ms.bitcast(U32), 1, None, ALU.logical_shift_right))
            link(V.tensor_scalar(y_.bitcast(I32), y_.bitcast(I32), -1.0, float(0x5F3759DF), ALU.mult, ALU.add))
            for _ in range(4):
                link(V.tensor_tensor(t_, y_, y_, ALU.mult))
                link(V.scalar_tensor_tensor(t_, t_, -0.5, ms, ALU.mult, ALU.mult))
                link(V.scalar_tensor_tensor(y_, t_, 1.5, y_, ALU.add, ALU.mult))
            dve.wait_ge(s_ready, TILES)
            for t in range(TILES):
                step(V.tensor_scalar(s_out[:, t, :], s_out[:, t, :], rms[:, 1, t:t + 1], None, ALU.mult))

            with dve.Fori(0, LAST) as i:
                for u in range(EPI):
                    expert_rows(i * EPI + u, i, u, True)
            for u in range(EPI):
                expert_rows(LAST * EPI + u, LAST, u, u + 1 < EPI)

            def add_choices(i):
                for k in range(CHOICES):
                    dve.wait_ge(moe_loaded[k][i], 16)
                t = slice(2 * i, 2 * i + 2)
                V.tensor_tensor(moe[:, 0, t, :], moe[:, 0, t, :], moe[:, 1, t, :], ALU.add).then_inc(moe_summed, 1)

            dve.wait_ge(dve_steps, chained[0])
            add_choices(0)
            for i in range(4):
                t = slice(2 * i, 2 * i + 2)
                if i + 1 < 4:
                    add_choices(i + 1)
                dve.wait_ge(moe_silu, i + 1)
                link(V.tensor_tensor(s_out[:, t, :], s_out[:, t, :], moe[:, 1, t, :], ALU.mult))
                V.tensor_tensor(s_out[:, t, :], s_out[:, t, :], x_sb[:, t, :], ALU.add).then_inc(out_ready, 1)

        @block.tensor
        def _(pe):
            T = nc.tensor

            pe.wait_ge(masks_ready, 8)
            for t in range(TILES):
                pe.wait_ge(xn_ready, t + 1)
                if t >= 2:
                    pe.wait_ge(xn_t_ready, t - 1)
                for k in range(KD):
                    last = T.transpose(bank[t % 2][:, k * P:(k + 1) * P], rec[:, 0, t, k * P:(k + 1) * P], ident[:, :])
                last.then_inc(xn_t_psum, 1)
            pe.wait_ge(small_loaded, 48)
            for t in range(TILES):
                pe.wait_ge(xn_t_ready, t + 1)
                for k in range(KD):
                    last = T.matmul(bank[3][:, t * NSMALL:(t + 1) * NSMALL], xn_t[:, k, t * P:(t + 1) * P],
                                    wsmall[:, k, :], start=(k == 0), stop=(k == KD - 1))
            last.then_inc(small_psum, 1)

            def place_products():
                pe.wait_ge(hot_ready, 1)
                q = CHOICES * TILES
                rows = hot[:, :, :]
                T.matmul(bank[2][:, 0:q * EXPERTS], before16[:, :], rows.rearrange("p q e -> p (q e)"),
                         start=True, stop=False)
                for n in range(q - 1):
                    dst = bank[2][:, (n + 1) * EXPERTS:q * EXPERTS].rearrange("p (q e) -> p q e", e=EXPERTS)
                    last = T.matmul(dst, ones16[:, :],
                                    hot[:, n, :].unsqueeze(1).to_broadcast([P, q - 1 - n, EXPERTS]),
                                    start=False, stop=(n == q - 2))
                last.then_inc(place_psum, 1)

            for i, (kind, m, n) in enumerate(PROJ):
                pe.wait_ge(win_loaded[0 if kind == "z" else 1], 16)
                if i == HT * SPANS:
                    place_products()
                if i >= 4:
                    before, mm, nn = PROJ[i - 4]
                    if before == "z":
                        pe.wait_ge(z_ready, i - 3)
                    else:
                        pe.wait_ge(conv_ready, convolved(mm, nn))
                c = col0(kind, m)
                for k in range(KD):
                    last = T.matmul(bank[PROJ_BANKS[i % 4]][:, :], win[:, k, c:c + P], xn_t[:, k, n * SPAN:(n + 1) * SPAN],
                                    start=(k == 0), stop=(k == KD - 1))
                last.then_inc(proj_psum, 1)

            pe.wait_ge(a_dt_ready, 1)
            pe.wait_ge(slots_known, 1)
            T.matmul(bank[2][:, 0:TILES * HEADS], later[:, :], a_dt[:, :, :].rearrange("p t h -> p (t h)"),
                     start=True, stop=True).then_inc(decay_psum, 1)

            def ssd_inputs(c):
                b = c % 2
                now = slice(c * P, (c + 1) * P)
                if c % TPS == 0:
                    pe.wait_ge(conv_read, (c // TPS + 1) * CTILES)
                    pe.wait_ge(c_moved[c // TPS], 16)
                if c >= 1:
                    pe.wait_ge(xs_ready, c)
                    pe.wait_ge(xd_ready, (c + 1) // 2)
                for h in range(HT):
                    last = T.transpose(bank[0][:, h * P:(h + 1) * P], xc[:, h, now], ident[:, :])
                last.then_inc(xt_psum, 1)
                if c >= 1:
                    pe.wait_ge(cb_ready, c)
                T.matmul(bank[1][:, 0:P], bc[0:STATE, now], c_low[:, now], start=True, stop=True).then_inc(cb_psum, 1)
                pe.wait_ge(steps_ready, c + 1)
                if c == 0:
                    pe.wait_ge(decay_ready, 1)
                else:
                    pe.wait_ge(seg_ready, c)
                step_row = steps[:, b, :, :].rearrange("p h l -> p (h l)")
                T.matmul(bank[2][:, :], later[:, :], step_row, start=True, stop=True).then_inc(seg_psum, 1)
                if b == 0:
                    if c >= 2:
                        pe.wait_ge(state_ready, c // 2)
                    T.transpose(bank[7][:, 0:P], bc[:, now], ident[:, :]).then_inc(b_tok_psum, 1)
                else:
                    if c >= 3:
                        pe.wait_ge(cexp_ready, c // 2)
                    T.matmul(bank[4][0:STATE, :], ones[:, :], step_row, start=True, stop=True).then_inc(cdec_psum, 1)

            def ssd_state(c):
                pe.wait_ge(xd_ready, c // 2 + 1)
                pe.wait_ge(b_tok_ready, c // 2 + 1)
                T.matmul(bank[7][0:STATE, :], b_tok[:, :], xd[:, :, :].rearrange("p h l -> p (h l)"),
                         start=True, stop=True).then_inc(state_psum, 1)

            def ssd_y(c):
                b = c % 2
                pe.wait_ge(xs_ready, c + 1)
                pe.wait_ge(mix_ready, c + 1)
                if b == 1:
                    pe.wait_ge(state_ready, c // 2 + 1)
                    pe.wait_ge(cdec_ready, c // 2 + 1)
                if c >= 1:
                    pe.wait_ge(y_read, HT * c)
                for h in range(HEADS):
                    dst = bank[3][:, h * P:(h + 1) * P]
                    last = T.matmul(dst, xs[:, b, h, :], seg[:, b, h, :], start=True, stop=(b == 0))
                    if b == 1:
                        last = T.matmul(dst, state[:, h, :], c_dec[:, h, :], start=False, stop=True)
                last.then_inc(y_psum, 1)

            def out_proj(c):
                b = c % 2
                if c == 0:
                    pe.wait_ge(wout_scaled, HT)
                else:
                    pe.wait_ge(s_ready, c)
                pe.wait_ge(g_ready, c + 1)
                for h in range(HT):
                    T.matmul(bank[5][:, 0:DM], g[:, b, h, :], wout[:, h, :], start=(h == 0), stop=(h == HT - 1))
                pe.wait_ge(gsq_ready, c + 1)
                for h in range(HT):
                    last = T.matmul(bank[6][:, c:c + 1], gsq[:, b, h, :], ones[:, 0:1], start=(h == 0), stop=(h == HT - 1))
                last.then_inc(s_psum, 1)

            ssd_inputs(0)
            for c in range(TILES):
                if c + 1 < TILES:
                    ssd_inputs(c + 1)
                if c % 2 == 0:
                    ssd_state(c)
                ssd_y(c)
                if c >= 1:
                    out_proj(c - 1)
            out_proj(TILES - 1)

            def slots_transposed(e, i, u):
                pe.wait_ge(slots_loaded[u], (i + 1) * 16)
                for k in range(KD):
                    for h in range(CH):
                        last = T.transpose(bank[0][:, k * CAP + h * P:k * CAP + (h + 1) * P],
                                           slots[:, u, h, k * P:(k + 1) * P], ident[:, :])
                last.then_inc(slots_t_psum, 1)

            def fc1(e, i, u):
                pe.wait_ge(slots_t_ready, e + 1)
                pe.wait_ge(w_loaded[0][u], (i + 1) * 16)
                for f in range(FT):
                    pe.wait_ge(hid_ready, e * FT + f + 1)
                    for k in range(KD):
                        last = T.matmul(bank[FC1_BANKS[f % NB1]][:, 0:CAP], w1[:, u, k, f * P:(f + 1) * P],
                                        slots_t[:, u, k, :], start=(k == 0), stop=(k == KD - 1))
                    last.then_inc(fc1_psum, 1)

            def fc2(e, i, u):
                pe.wait_ge(w_loaded[1][u], (i + 1) * 16)
                for h in range(CH):
                    pe.wait_ge(fc2_read, e * CH + h + 1)
                    for f in range(FT):
                        if h == 0:
                            pe.wait_ge(hid_ready, NB1 + e * FT + f + 1)
                        last = T.matmul(bank[FC2_BANKS[h]][:, 0:DM], hid[:, f, h * P:(h + 1) * P], w2[:, u, f, :],
                                        start=(f == 0), stop=(f == FT - 1))
                    last.then_inc(fc2_psum, 1)

            def expert(e, i, u, follow):
                fc1(e, i, u)
                if follow:
                    slots_transposed(e + 1, i + u, 1 - u)
                fc2(e, i, u)

            slots_transposed(0, 0, 0)
            pe.wait_ge(y_read, HT * TILES)
            pe.wait_ge(s_ready, TILES)
            pe.sem_inc(hid_ready, NB1)
            pe.sem_inc(fc2_read, CH)
            with pe.Fori(0, LAST) as i:
                for u in range(EPI):
                    expert(i * EPI + u, i, u, True)
            for u in range(EPI):
                expert(LAST * EPI + u, LAST, u, u + 1 < EPI)


def kernel(**inputs):
    import numpy as np
    import concourse.bacc as bacc
    from concourse.bass_utils import run_bass_kernel_spmd

    a = {k.split("_", 2)[2]: np.asarray(v) for k, v in inputs.items()}
    di, heads, taps = a["W_out"].shape[1], a["A_log"].shape[0], a["W_conv"].shape[2]
    w_in_t = np.ascontiguousarray(a["W_in"].T)
    small0 = w_in_t.shape[1] - heads
    ctiles = a["W_conv"].shape[0] // P
    channels = np.concatenate([
        a["W_conv"].reshape(ctiles, P, taps).transpose(1, 0, 2).reshape(P, ctiles * taps),
        a["b_conv"].reshape(ctiles, P).T, a["norm_w"].reshape(di // P, P).T], axis=1)
    e, hidden = a["fc1_b"].shape
    arrays = {
        "x": a["u"].reshape(-1, a["u"].shape[-1]),
        "w_in_t": w_in_t,
        "w_small": np.concatenate([w_in_t[:, small0:], a["wg"]], axis=1),
        "head_params": np.concatenate([a["dt_bias"], a["A_log"], a["D"]])[None],
        "channel_params": channels,
        "w_out_t": a["W_out"].T,
        "fc1_w": a["fc1_w"],
        "fc1_b": a["fc1_b"].reshape(e, hidden // P, P).transpose(0, 2, 1),
        "fc2_w": a["fc2_w"],
        "fc2_b": a["fc2_b"],
    }
    arrays = {k: np.ascontiguousarray(v) for k, v in arrays.items()}
    nc = bacc.Bacc("TRN2", target_bir_lowering=False, num_devices=1)
    args = [nc.dram_tensor(k, v.shape, mybir.dt.from_np(v.dtype), kind="ExternalInput").ap() for k, v in arrays.items()]
    args.append(nc.dram_tensor("out", arrays["x"].shape, F32, kind="ExternalOutput").ap())
    layer(nc, *args)
    r = run_bass_kernel_spmd(nc, [arrays], core_ids=[0])
    return r.results[0]["out"].reshape(a["u"].shape)
```

```python
from contextlib import ExitStack

import concourse.bass as bass
from concourse import mybir

F32 = mybir.dt.float32
BF16 = mybir.dt.bfloat16
I32 = mybir.dt.int32
U32 = mybir.dt.uint32
ALU = mybir.AluOpType
ACT = mybir.ActivationFunctionType
AX_X = mybir.AxisListType.X

P = 128
TAPS = 4
EPS = 1e-5
DROPPED = float(1 << 20)


def layer(nc, x, w_in_t, w_small, head_params, channel_params, w_out_t,
          fc1_w, fc1_b, fc2_w, fc2_b, out):
    TOKENS, DM = x.shape
    KD = DM // P
    TILES = TOKENS // P
    HEADS = head_params.shape[1] // 3
    DI = w_out_t.shape[0]
    HT = DI // P
    STATE = (w_in_t.shape[1] - 2 * DI - HEADS) // 2
    EXPERTS, _, HIDDEN = fc1_w.shape
    FT = HIDDEN // P
    CHOICES = 2
    CAP = CHOICES * TOKENS // EXPERTS
    SLOTS = EXPERTS * CAP
    CH = CAP // P
    REC = DM + 2
    SPAN = 512
    SPANS = TOKENS // SPAN
    TPS = SPAN // P
    SEQ = 256
    NSMALL = HEADS + EXPERTS
    CTILES = HT + 1
    assert HT == HEADS and STATE == 64 and CH == 2 and KD == 2

    slots_dram = nc.dram_tensor("expert_slots", [SLOTS, REC], F32).ap()
    moe_dram = nc.dram_tensor("moe_rows", [TOKENS, DM], F32).ap()

    with ExitStack() as ctx:
        def sb(name, shape, dt=F32):
            return ctx.enter_context(nc.sbuf_tensor(name, shape, dt))

        def sem(name):
            return ctx.enter_context(nc.semaphore(name))

        bank = [ctx.enter_context(nc.psum_tensor(f"bank{i}", [P, 512], F32)) for i in range(8)]

        x_sb = sb("x_sb", [P, TILES, DM])
        rec = sb("rec", [P, CHOICES, TILES, REC])
        xn_t = sb("xn_t", [P, KD, TOKENS])
        win = sb("win", [P, KD, w_in_t.shape[1]])
        wsmall = sb("wsmall", [P, KD, NSMALL])
        heads = sb("heads", [P, 3 * HEADS])
        chan = sb("chan", [P, CTILES * TAPS + CTILES + HT])
        wout = sb("wout", [P, HT, DM])
        zs = sb("zs", [P, HT, TOKENS])
        xc = sb("xc", [P, HT, TOKENS])
        bc = sb("bc", [P, TOKENS])
        c_low = sb("c_low", [STATE, TOKENS])
        conv = sb("conv", [P, 4, SPAN])
        ident = sb("ident", [P, P])
        later = sb("later", [P, P])
        upto = sb("upto", [P, P])
        ones = sb("ones", [P, STATE])
        before16 = sb("before16", [P, P], BF16)
        ones16 = sb("ones16", [P, P], BF16)
        zeros = sb("zeros", [P, 4 * REC])
        prefer = sb("prefer", [P, EXPERTS])
        slot0 = sb("slot0", [P, CHOICES * TILES, EXPERTS])
        bn = sb("bn", [P, TILES, 6])
        mv = sb("mv", [P, TILES, 2])
        std = sb("std", [P, TILES])
        rstd = sb("rstd", [P, TILES])
        shift = sb("shift", [P, TILES])
        lg = sb("lg", [P, TILES, EXPERTS])
        ex = sb("ex", [P, TILES, EXPERTS])
        sc = sb("sc", [P, CHOICES, TILES, EXPERTS])
        key = sb("key", [P, TILES, EXPERTS])
        stat = sb("stat", [P, 10, TILES])
        hot = sb("hot", [P, CHOICES * TILES, EXPERTS], BF16)
        place = sb("place", [P, 3, CHOICES * TILES, EXPERTS])
        slot_f = sb("slot_f", [P, CHOICES * TILES])
        slot_i = sb("slot_i", [P, CHOICES * TILES], I32)
        dtw = sb("dtw", [P, 10, TILES, HEADS])
        a_exp = sb("a_exp", [P, HEADS])
        a_dt = sb("a_dt", [P, TILES, HEADS])
        dt_sb = sb("dt_sb", [P, TILES, HEADS])
        decay = sb("decay", [P, TILES, HEADS])
        a_upto = sb("a_upto", [P, HEADS, P])
        x_chunk = sb("x_chunk", [P, HT, P])
        bc_chunk = sb("bc_chunk", [P, P])
        mix = sb("mix", [P, HEADS, P])
        cb = sb("cb", [P, P])
        xs = sb("xs", [P, HEADS, P])
        xd = sb("xd", [P, HEADS, P])
        b_tok = sb("b_tok", [P, STATE])
        state = sb("state", [STATE, HEADS, P])
        c_dec = sb("c_dec", [STATE, HEADS, P])
        g = sb("g", [P, HT, P])
        gsq = sb("gsq", [P, HT, P])
        gsum = sb("gsum", [P, P])
        s_out = sb("s_out", [P, TILES, DM + 1])
        rms = sb("rms", [P, 4, TILES])
        w1 = sb("w1", [P, 2, KD, HIDDEN])
        w2 = sb("w2", [P, 2, FT, DM])
        b1 = sb("b1", [P, 2, FT])
        b2 = sb("b2", [P, 2, DM])
        slots = sb("slots", [P, 2, CH, REC])
        slots_t = sb("slots_t", [P, 2, KD, CAP])
        hid = sb("hid", [P, FT, CAP])
        eo = sb("eo", [P, 2, CH, DM])
        gate = sb("gate", [P, 2, CH])
        row_t = sb("row_t", [P, CH])
        row_i = sb("row_i", [P, 2, CH], I32)
        moe = w1[:, :, :, :].rearrange("p u k f -> p u (k f)").rearrange("p u (t c) -> p u t c", c=DM)

        x_loaded = [sem(f"x_loaded{i}") for i in range(2)]
        small_loaded = sem("small_loaded")
        win_loaded = [sem(f"win_loaded{i}") for i in range(2)]
        wout_loaded = sem("wout_loaded")
        zeros_ready = sem("zeros_ready")
        dram_cleared = sem("dram_cleared")
        masks_ready = sem("masks_ready")
        pool_steps = sem("pool_steps")
        router_steps = sem("router_steps")
        dt_steps = sem("dt_steps")
        dve_steps = sem("dve_steps")
        var_ready = sem("var_ready")
        std_ready = sem("std_ready")
        xn_ready = [sem(f"xn_ready{i}") for i in range(2)]
        shift_ready = sem("shift_ready")
        rec_copied = sem("rec_copied")
        xn_t_psum = sem("xn_t_psum")
        xn_t_ready = sem("xn_t_ready")
        small_psum = sem("small_psum")
        exp_in_ready = sem("exp_in_ready")
        exp_out_ready = sem("exp_out_ready")
        hot_ready = sem("hot_ready")
        place_psum = sem("place_psum")
        slots_known = sem("slots_known")
        gates_ready = sem("gates_ready")
        scattered = [sem(f"scattered{i}") for i in range(4)]
        proj_psum = sem("proj_psum")
        proj_read = sem("proj_read")
        tap_ready = sem("tap_ready")
        conv_steps = sem("conv_steps")
        conv_ready = sem("conv_ready")
        conv_read = sem("conv_read")
        z_ready = sem("z_ready")
        c_moved = [sem(f"c_moved{i}") for i in range(SPANS)]
        a_dt_ready = sem("a_dt_ready")
        decay_psum = sem("decay_psum")
        decay_ready = sem("decay_ready")
        decay_used = sem("decay_used")
        a_upto_ready = sem("a_upto_ready")
        chunk_staged = sem("chunk_staged")
        wout_scaled = sem("wout_scaled")
        xt_psum = sem("xt_psum")
        xs_ready = sem("xs_ready")
        xd_ready = sem("xd_ready")
        cb_psum = sem("cb_psum")
        cb_ready = sem("cb_ready")
        seg_psum = sem("seg_psum")
        seg_ready = sem("seg_ready")
        mix_ready = sem("mix_ready")
        last_in_psum = sem("last_in_psum")
        b_tok_ready = sem("b_tok_ready")
        cexp_ready = sem("cexp_ready")
        cdec_ready = sem("cdec_ready")
        state_psum = sem("state_psum")
        state_ready = sem("state_ready")
        y_psum = sem("y_psum")
        y_read = sem("y_read")
        g_ready = sem("g_ready")
        gsq_ready = sem("gsq_ready")
        gsum_ready = sem("gsum_ready")
        s_psum = sem("s_psum")
        s_ready = sem("s_ready")
        w_loaded = [[sem(f"w{j}_loaded{u}") for u in range(2)] for j in (1, 2)]
        bias_loaded = [sem(f"bias_loaded{u}") for u in range(2)]
        slots_loaded = [sem(f"slots_loaded{u}") for u in range(2)]
        slots_t_psum = sem("slots_t_psum")
        slots_t_ready = sem("slots_t_ready")
        fc1_psum = sem("fc1_psum")
        hid_ready = sem("hid_ready")
        fc2_psum = sem("fc2_psum")
        fc2_read = sem("fc2_read")
        row_step = sem("row_step")
        slot_info = sem("slot_info")
        eo_ready = sem("eo_ready")
        eo_free = sem("eo_free")
        rows_scattered = [[sem(f"rows_scattered{u}{h}") for h in range(CH)] for u in range(2)]
        moe_loaded = [sem(f"moe_loaded{i}") for i in range(4)]
        moe_silu = sem("moe_silu")
        out_ready = sem("out_ready")
        stored = sem("stored")

        x_v = x.rearrange("(t p) d -> p t d", p=P)
        out_v = out.rearrange("(t p) d -> p t d", p=P)
        moe_v = moe_dram.rearrange("(t p) d -> p t d", p=P)
        slots_v = slots_dram.rearrange("(e h p) r -> e p h r", p=P, h=CH)
        win_v = w_in_t.rearrange("(k p) c -> p k c", p=P)
        w1_v = fc1_w.rearrange("e (k p) f -> e p k f", p=P)
        w2_v = fc2_w.rearrange("e (f p) d -> e p f d", p=P)
        HALF = TILES // 2
        STEPS = EXPERTS
        assert STEPS == TILES
        dt_bias = heads[:, 0:HEADS]
        a_log = heads[:, HEADS:2 * HEADS]

        def d_skip(h):
            return heads[:, 2 * HEADS + h:2 * HEADS + h + 1]

        def tap(c, j):
            return chan[:, c * TAPS + j:c * TAPS + j + 1]

        def conv_bias(c):
            return chan[:, CTILES * TAPS + c:CTILES * TAPS + c + 1]

        def norm_w(h):
            return chan[:, CTILES * TAPS + CTILES + h:CTILES * TAPS + CTILES + h + 1]

        Z = [("z", m, n) for n in range(SPANS) for m in range(HT)]
        X = [("xbc", m, n) for n in range(SPANS) for m in [HT] + list(range(HT))]
        PROJ = Z[0:5] + X[0:8] + Z[5:7] + X[8:10]+Z[7:]
        PROJ_BANKS = [0, 1, 4, 5, 6, 7]
        NPB = len(PROJ_BANKS)
        WARM_UP = 14
        DECAY_AT = 6
        PLACES_AT = 5
        XBC = [(i, m, n) for i, (kind, m, n) in enumerate(PROJ) if kind == "xbc"]
        TRANSPOSED, FC1_BANKS, FC2_BANKS, SEG, CB_THEN_Y, OUT_THEN_STATE = 0, [1, 2], [3, 4], 5, 6, 7
        NB1 = len(FC1_BANKS)

        def col0(kind, m):
            return m * P if kind == "z" else DI + m * P

        def convolved(c, n):
            return next(j for j, (_, m, nn) in enumerate(XBC) if (m, nn) == (c, n)) + 1

        block = ctx.enter_context(nc.Block())

        @block.sync
        def _(sp):
            for i in range(2):
                half = slice(i * HALF, (i + 1) * HALF)
                sp.dma_start(x_sb[:, half, :], x_v[:, half, :]).then_inc(x_loaded[i], 16)
            for n in range(2):
                c = slice(n * DI, DI if n == 0 else w_in_t.shape[1])
                sp.dma_start(win[:, :, c], win_v[:, :, c]).then_inc(win_loaded[n], 16)
            sp.wait_ge(zeros_ready, 1)
            for i in range(SLOTS // (4 * P)):
                dst = slots_dram[i * 4 * P:(i + 1) * 4 * P, :].rearrange("(p r) c -> p (r c)", p=P)
                sp.dma_start(dst, zeros[:, :]).then_inc(dram_cleared, 16)
            for i in range(TOKENS // (4 * P)):
                dst = moe_dram[i * 4 * P:(i + 1) * 4 * P, :].rearrange("(p r) c -> p (r c)", p=P)
                sp.dma_start(dst, zeros[:, 0:4 * DM]).then_inc(dram_cleared, 16)
            sp.dma_start(wout[:, :, :], w_out_t.rearrange("(h p) d -> p h d", p=P)).then_inc(wout_loaded, 16)

            def load_weights(e, u):
                sp.dma_start(w1[:, u, :, :], w1_v[e:e + 1].rearrange("e p k f -> (e p) k f")
                             ).then_inc(w_loaded[0][u], 16)
                sp.dma_start(w2[:, u, :, :], w2_v[e:e + 1].rearrange("e p f d -> (e p) f d")
                             ).then_inc(w_loaded[1][u], 16)
                sp.dma_start(b1[:, u, :], fc1_b[e:e + 1].rearrange("e p f -> (e p) f")
                             ).then_inc(bias_loaded[u], 16)
                sp.dma_start(b2[:, u, :], fc2_b[e:e + 1].to_broadcast([P, DM])
                             ).then_inc(bias_loaded[u], 16)

            def load_slots(e, u):
                sp.dma_start(slots[:, u, :, :], slots_v[e:e + 1].rearrange("e p h r -> (e p) h r")
                             ).then_inc(slots_loaded[u], 16)

            load_weights(0, 0)
            load_weights(1, 1)
            for s in scattered:
                sp.wait_ge(s, 16 * CHOICES * TILES // 4)
            load_slots(0, 0)
            load_slots(1, 1)
            for e in range(STEPS - 2):
                sp.wait_ge(slots_t_psum, e + 1)
                sp.wait_ge(slot_info, e + 1)
                load_slots(e + 2, e % 2)
                sp.wait_ge(fc2_psum, (e + 1) * CH)
                sp.wait_ge(fc2_read, CH + (e + 1) * CH)
                load_weights(e + 2, e % 2)

            for u in range(2):
                for h in range(CH):
                    sp.wait_ge(rows_scattered[u][h], 16 * STEPS // 2)
            for i in range(4):
                t = slice(2 * i, 2 * i + 2)
                sp.dma_start(moe[:, 0, t, :], moe_v[:, t, :]).then_inc(moe_loaded[i], 16)
            for i in range(4):
                t = slice(2 * i, 2 * i + 2)
                sp.wait_ge(out_ready, i + 1)
                sp.dma_start(out_v[:, t, :], moe[:, 0, t, :]).then_inc(stored, 16)
            sp.wait_ge(stored, 64)

        @block.gpsimd
        def _(pool):
            done = [0]

            def step(ins):
                done[0] += 1
                return ins.then_inc(pool_steps, 1)

            nc.gpsimd.memset(zeros[:, :], 0.0).then_inc(zeros_ready, 1)
            step(nc.gpsimd.memset(ident[:, :], 0.0))
            step(nc.gpsimd.memset(later[:, :], 1.0))
            step(nc.gpsimd.memset(upto[:, :], 1.0))
            step(nc.gpsimd.memset(before16[:, :], 1.0))
            pool.wait_ge(pool_steps, 4)
            nc.gpsimd.affine_select(out=ident[:, :], in_=ident[:, :], compare_op=ALU.not_equal, fill=1.0,
                                    base=0, pattern=[[-1, P]], channel_multiplier=1).then_inc(masks_ready, 1)
            nc.gpsimd.affine_select(out=before16[:, :], in_=before16[:, :], compare_op=ALU.is_gt, fill=0.0,
                                    base=0, pattern=[[1, P]], channel_multiplier=-1).then_inc(masks_ready, 1)
            nc.gpsimd.memset(ones16[:, :], 1.0).then_inc(masks_ready, 1)
            nc.gpsimd.iota(prefer[:, :], pattern=[[-1, EXPERTS]], base=EXPERTS, channel_multiplier=0,
                           allow_small_or_imprecise_dtypes=True).then_inc(masks_ready, 1)
            nc.gpsimd.iota(slot0[:, :, :], pattern=[[0, CHOICES * TILES], [CAP, EXPERTS]], base=0,
                           channel_multiplier=0, allow_small_or_imprecise_dtypes=True).then_inc(masks_ready, 1)
            nc.gpsimd.affine_select(out=later[:, :], in_=later[:, :], compare_op=ALU.is_gt, fill=0.0,
                                    base=0, pattern=[[-1, P]], channel_multiplier=1).then_inc(masks_ready, 1)
            nc.gpsimd.affine_select(out=upto[:, :], in_=upto[:, :], compare_op=ALU.is_ge, fill=0.0,
                                    base=0, pattern=[[1, P]], channel_multiplier=-1).then_inc(masks_ready, 1)
            nc.gpsimd.memset(ones[:, :], 1.0).then_inc(masks_ready, 1)
            for k in range(CHOICES):
                nc.gpsimd.iota(rec[:, k, :, DM + 1], pattern=[[P, TILES]], base=1,
                               channel_multiplier=1, allow_small_or_imprecise_dtypes=True
                               ).then_inc(rec_copied, 1)
            for t in range(TILES):
                pool.wait_ge(xn_ready[t % 2], t // 2 + 1)
                nc.gpsimd.tensor_copy(rec[:, 1, t, 0:DM], rec[:, 0, t, 0:DM]).then_inc(rec_copied, 1)
            pool.wait_ge(rec_copied, CHOICES + TILES)
            pool.wait_ge(gates_ready, CHOICES)
            pool.wait_ge(slots_known, 1)
            pool.wait_ge(dram_cleared, 16 * (SLOTS + TOKENS) // (4 * P))
            for q in range(CHOICES * TILES):
                k, t = divmod(q, TILES)
                nc.gpsimd.indirect_dma_start(
                    out=slots_dram, out_offset=bass.IndirectOffsetOnAxis(ap=slot_i[:, q:q + 1].bitcast(U32), axis=0),
                    in_=rec[:, k, t, :], in_offset=None, bounds_check=SLOTS - 1, oob_is_err=False,
                ).then_inc(scattered[q % 4], 16)

            def stage(n):
                now = slice(n * P, (n + 1) * P)
                if n % TPS == 0:
                    pool.wait_ge(conv_read, (n // TPS + 1) * CTILES)
                if n >= 1:
                    pool.wait_ge(last_in_psum, n)
                nc.gpsimd.tensor_copy(x_chunk[:, :, :], xc[:, :, now]).then_inc(chunk_staged, 1)
                nc.gpsimd.tensor_copy(bc_chunk[:, :], bc[:, now]).then_inc(chunk_staged, 1)
                nc.gpsimd.tensor_tensor(
                    a_upto[:, :, :], a_dt[:, n, :].unsqueeze(2).to_broadcast([P, HEADS, P]),
                    upto[:, :].unsqueeze(1).to_broadcast([P, HEADS, P]), ALU.mult).then_inc(a_upto_ready, 1)

            pool.wait_ge(wout_loaded, 16)
            pool.wait_ge(small_loaded, 48)
            for h in range(HT):
                nc.gpsimd.tensor_scalar(wout[:, h, :], wout[:, h, :], norm_w(h), None, ALU.mult
                                        ).then_inc(wout_scaled, 1)

            pool.wait_ge(a_dt_ready, 1)
            stage(0)
            for e in range(STEPS):
                if e + 1 < STEPS:
                    stage(e + 1)
                u = e % 2
                for h in range(CH):
                    pool.wait_ge(eo_ready, e * CH + h + 1)
                    nc.gpsimd.indirect_dma_start(
                        out=moe_dram,
                        out_offset=bass.IndirectOffsetOnAxis(ap=row_i[:, u, h:h + 1].bitcast(U32), axis=0),
                        in_=eo[:, u, h, :], in_offset=None, bounds_check=TOKENS - 1,
                        oob_is_err=False, compute_op=ALU.add).then_inc(rows_scattered[u][h], 16)
                for h in range(CH):
                    pool.wait_ge(rows_scattered[u][h], 16 * (e // 2 + 1))
                pool.sem_inc(eo_free, 1)

        @block.scalar
        def _(act):
            act.dma_start(wsmall[:, :, :], w_small.rearrange("(k p) c -> p k c", p=P)).then_inc(small_loaded, 16)
            act.dma_start(heads[:, :], head_params[0:1, :].to_broadcast([P, 3 * HEADS])).then_inc(small_loaded, 16)
            act.dma_start(chan[:, :], channel_params).then_inc(small_loaded, 16)
            def act_transposed(t):
                act.wait_ge(xn_t_psum, t + 1)
                nc.scalar.copy(xn_t[:, :, t * P:(t + 1) * P],
                               bank[t % 2][:, 0:KD * P].rearrange("p (k c) -> p k c", k=KD)).then_inc(xn_t_ready, 1)

            for i in range(2):
                half = slice(i * HALF, (i + 1) * HALF)
                act.wait_ge(var_ready, i + 1)
                nc.scalar.activation(std[:, half], stat[:, 9, half], ACT.Sqrt).then_inc(std_ready, 1)
                act.wait_ge(shift_ready, i + 1)
                for t in range(i * HALF + 1, (i + 1) * HALF, 2):
                    nc.scalar.activation(rec[:, 0, t, 0:DM], x_sb[:, t, :], ACT.Identity, bias=shift[:, t:t + 1],
                                         scale=rstd[:, t:t + 1]).then_inc(xn_ready[1], 1)
                for t in range(i * HALF, (i + 1) * HALF):
                    act_transposed(t)
            act.wait_ge(small_loaded, 48)
            nc.scalar.activation(a_exp[:, :], a_log, ACT.Exp).then_inc(exp_out_ready, 1)
            act.wait_ge(exp_in_ready, 1)
            nc.scalar.activation(ex[:, :, :], lg[:, :, :], ACT.Exp).then_inc(exp_out_ready, 1)
            act.wait_ge(exp_in_ready, 2)
            nc.scalar.activation(dtw[:, 2, :, :], dtw[:, 1, :, :], ACT.Exp).then_inc(exp_out_ready, 1)

            def conv_silu(j):
                _, m, n = XBC[j]
                act.wait_ge(conv_ready, j + 1)
                dst = bc[:, n * SPAN:(n + 1) * SPAN] if m == HT else xc[:, m, n * SPAN:(n + 1) * SPAN]
                nc.scalar.activation(dst, conv[:, j % 4, :], ACT.Silu, bias=conv_bias(m)).then_inc(conv_read, 1)
                if m == HT:
                    act.wait_ge(conv_read, j + 1)
                    act.dma_start(c_low[:, n * SPAN:(n + 1) * SPAN], bc[STATE:2 * STATE, n * SPAN:(n + 1) * SPAN]
                                  ).then_inc(c_moved[n], 16)

            j = 0
            for i, (kind, m, n) in enumerate(PROJ):
                if i == PLACES_AT + 4:
                    act.wait_ge(decay_psum, 1)
                    nc.scalar.activation(decay[:, :, :], bank[2][:, 0:TILES * HEADS].rearrange("p (t h) -> p t h", h=HEADS),
                                         ACT.Exp).then_inc(decay_ready, 1)
                src = bank[PROJ_BANKS[i % NPB]]
                if kind == "z":
                    act.wait_ge(proj_psum, i + 1)
                    nc.scalar.activation(zs[:, m, n * SPAN:(n + 1) * SPAN], src[:, :], ACT.Silu).then_inc(z_ready, 1)
                else:
                    if j >= 4:
                        conv_silu(j - 4)
                        act.wait_ge(conv_read, j - 3)
                    act.wait_ge(proj_psum, i + 1)
                    nc.scalar.activation(conv[:, j % 4, :], src[:, :], ACT.Copy, scale=tap(m, TAPS - 1)
                                         ).then_inc(tap_ready, 1)
                    j += 1
            for j in range(len(XBC) - 4, len(XBC)):
                conv_silu(j)

            def act_step(n, pair, u, first=False):
                act.wait_ge(bias_loaded[u], (pair + 1) * 32)
                for f in range(FT):
                    act.wait_ge(fc1_psum, n * FT + f + 1)
                    nc.scalar.activation(hid[:, f, :], bank[FC1_BANKS[f % NB1]][:, 0:CAP], ACT.Gelu,
                                         bias=b1[:, u, f:f + 1]).then_inc(hid_ready, 1)
                    if f == 2 and not first:
                        act_square(n - 1)
                if not first:
                    act_store(n - 1)
                act.wait_ge(seg_psum, n + 1)
                nc.scalar.activation(mix[:, :, :], bank[SEG][:, :].rearrange("p (h l) -> p h l", h=HEADS),
                                     ACT.Exp).then_inc(seg_ready, 1)
                act.wait_ge(last_in_psum, n + 1)
                low = bank[OUT_THEN_STATE][0:STATE, :].rearrange("p (h l) -> p h l", h=HEADS)
                if u == 0:
                    nc.scalar.copy(b_tok[:, :], bank[OUT_THEN_STATE][:, 0:STATE]).then_inc(b_tok_ready, 1)
                    act.wait_ge(state_psum, pair + 1)
                    nc.scalar.copy(state[:, :, :], low).then_inc(state_ready, 1)
                else:
                    nc.scalar.activation(c_dec[:, :, :], low, ACT.Exp).then_inc(cexp_ready, 1)

            def act_square(n):
                act.wait_ge(g_ready, n + 1)
                nc.scalar.square(gsq[:, :, :], g[:, :, :]).then_inc(gsq_ready, 1)

            def act_store(n):
                act.wait_ge(s_psum, n + 1)
                nc.scalar.copy(s_out[:, bass.ds(n, 1), :].rearrange("p a c -> p (a c)"),
                               bank[OUT_THEN_STATE][:, 0:DM + 1]).then_inc(s_ready, 1)

            act_step(0, 0, 0, first=True)
            with act.Fori(0, STEPS // 2 - 1) as i:
                act_step(i * 2 + 1, i, 1)
                act_step(i * 2 + 2, i + 1, 0)
            act_step(STEPS - 1, STEPS // 2 - 1, 1)
            act_square(STEPS - 1)
            act_store(STEPS - 1)

            for i in range(4):
                t = slice(2 * i, 2 * i + 2)
                act.wait_ge(moe_loaded[i], 16)
                nc.scalar.activation(moe[:, 1, t, :], moe[:, 0, t, :], ACT.Silu).then_inc(moe_silu, 1)

        @block.vector
        def _(dve):
            chained = [0]

            def link(ins):
                chained[0] += 1
                ins.then_inc(dve_steps, 1)
                dve.wait_ge(dve_steps, chained[0])

            def step(ins):
                chained[0] += 1
                ins.then_inc(dve_steps, 1)

            V = nc.vector

            def stats(i):
                dve.wait_ge(x_loaded[i], 16)
                for t in range(i * HALF, (i + 1) * HALF):
                    step(V.bn_stats(bn[:, t, :], x_sb[:, t, :]))
                dve.wait_ge(dve_steps, chained[0])
                for t in range(i * HALF, (i + 1) * HALF):
                    step(V.bn_aggr(mv[:, t, :], bn[:, t, :]))
                dve.wait_ge(dve_steps, chained[0])
                half = slice(i * HALF, (i + 1) * HALF)
                V.tensor_scalar(stat[:, 9, half], mv[:, half, 1], EPS, None, ALU.add).then_inc(var_ready, 1)

            def normalise(i):
                half = slice(i * HALF, (i + 1) * HALF)
                dve.wait_ge(std_ready, i + 1)
                link(V.reciprocal(rstd[:, half], std[:, half]))
                V.scalar_tensor_tensor(shift[:, half], mv[:, half, 0], -1.0, rstd[:, half], ALU.mult, ALU.mult
                                       ).then_inc(shift_ready, 1)
                for t in range(i * HALF, (i + 1) * HALF, 2):
                    V.tensor_scalar(rec[:, 0, t, 0:DM], x_sb[:, t, :], mv[:, t, 0:1], rstd[:, t:t + 1],
                                    ALU.subtract, ALU.mult).then_inc(xn_ready[0], 1)

            stats(0)
            normalise(0)
            stats(1)
            normalise(1)

            def over_e(a):
                return a.unsqueeze(2).to_broadcast([P, a.shape[1], EXPERTS])

            small = bank[3][:, 0:TILES * NSMALL].rearrange("p (t c) -> p t c", c=NSMALL)
            logits = small[:, :, HEADS:NSMALL]
            scores = [sc[:, k, :, :] for k in range(CHOICES)]
            hots = [hot[:, k * TILES:(k + 1) * TILES, :] for k in range(CHOICES)]
            top = [stat[:, 3 + k, :] for k in range(CHOICES)]
            preferred = prefer[:, :].unsqueeze(1).to_broadcast([P, TILES, EXPERTS])
            e_, d_, z_, z2, p_ = (dtw[:, n, :, :] for n in (2, 3, 4, 5, 6))
            dve.wait_ge(small_psum, 1)
            dve.wait_ge(small_loaded, 48)
            dve.wait_ge(masks_ready, 8)
            r_count, d_count = [0], [0]

            def r(ins):
                r_count[0] += 1
                ins.then_inc(router_steps, 1)

            def d(ins):
                d_count[0] += 1
                ins.then_inc(dt_steps, 1)

            def after_r():
                dve.wait_ge(router_steps, r_count[0])

            def after_d():
                dve.wait_ge(dt_steps, d_count[0])

            r(V.tensor_reduce(stat[:, 0, :], logits, AX_X, ALU.max))
            d(V.tensor_tensor(dtw[:, 0, :, :], small[:, :, 0:HEADS],
                              dt_bias.unsqueeze(1).to_broadcast([P, TILES, HEADS]), ALU.add))
            after_r()
            V.tensor_tensor(lg[:, :, :], logits, over_e(stat[:, 0, :]), ALU.subtract).then_inc(exp_in_ready, 1)
            after_d()
            V.scalar_tensor_tensor(dtw[:, 1, :, :], dtw[:, 0, :, :], -1.0, dtw[:, 0, :, :],
                                   ALU.mult, ALU.min).then_inc(exp_in_ready, 1)
            d(V.tensor_scalar(dtw[:, 7, :, :], dtw[:, 0, :, :], 0.0, None, ALU.max))
            dve.wait_ge(exp_out_ready, 2)
            r(V.tensor_reduce(stat[:, 1, :], ex[:, :, :], AX_X, ALU.add))
            dve.wait_ge(exp_out_ready, 3)
            d(V.tensor_scalar(d_, e_, 2.0, None, ALU.add))
            after_r()
            r(V.reciprocal(stat[:, 2, :], stat[:, 1, :]))
            after_d()
            d(V.reciprocal(d_, d_))
            after_r()
            r(V.tensor_tensor(scores[0], ex[:, :, :], over_e(stat[:, 2, :]), ALU.mult))
            after_d()
            d(V.tensor_tensor(z_, e_, d_, ALU.mult))
            after_r()
            r(V.tensor_reduce(top[0], scores[0], AX_X, ALU.max))
            after_d()
            d(V.tensor_tensor(z2, z_, z_, ALU.mult))
            after_r()
            r(V.tensor_tensor(key[:, :, :], scores[0], over_e(top[0]), ALU.is_equal))
            after_d()
            d(V.tensor_scalar(p_, z2, 1.0 / 17, None, ALU.mult))
            after_r()
            r(V.tensor_tensor(key[:, :, :], key[:, :, :], preferred, ALU.mult))
            after_d()
            d(V.scalar_tensor_tensor(p_, p_, 1.0 / 15, z2, ALU.add, ALU.mult))
            after_r()
            r(V.tensor_reduce(stat[:, 5, :], key[:, :, :], AX_X, ALU.max))
            after_d()
            d(V.scalar_tensor_tensor(p_, p_, 1.0 / 13, z2, ALU.add, ALU.mult))
            after_r()
            r(V.tensor_tensor(hots[0], key[:, :, :], over_e(stat[:, 5, :]), ALU.is_equal))
            after_d()
            d(V.scalar_tensor_tensor(p_, p_, 1.0 / 11, z2, ALU.add, ALU.mult))
            after_r()
            r(V.scalar_tensor_tensor(scores[1], hots[0], -2.0, scores[0], ALU.mult, ALU.add))
            after_d()
            d(V.scalar_tensor_tensor(p_, p_, 1.0 / 9, z2, ALU.add, ALU.mult))
            after_r()
            r(V.tensor_reduce(top[1], scores[1], AX_X, ALU.max))
            after_d()
            d(V.scalar_tensor_tensor(p_, p_, 1.0 / 7, z2, ALU.add, ALU.mult))
            after_r()
            r(V.tensor_tensor(key[:, :, :], scores[1], over_e(top[1]), ALU.is_equal))
            after_d()
            d(V.scalar_tensor_tensor(p_, p_, 1.0 / 5, z2, ALU.add, ALU.mult))
            after_r()
            r(V.tensor_tensor(key[:, :, :], key[:, :, :], preferred, ALU.mult))
            after_d()
            d(V.scalar_tensor_tensor(p_, p_, 1.0 / 3, z2, ALU.add, ALU.mult))
            after_r()
            r(V.tensor_reduce(stat[:, 5, :], key[:, :, :], AX_X, ALU.max))
            after_d()
            d(V.scalar_tensor_tensor(p_, p_, 1.0, z_, ALU.add, ALU.mult))
            after_r()
            V.tensor_tensor(hots[1], key[:, :, :], over_e(stat[:, 5, :]), ALU.is_equal).then_inc(hot_ready, 1)
            after_d()
            d(V.scalar_tensor_tensor(dt_sb[:, :, :], p_, 2.0, dtw[:, 7, :, :], ALU.mult, ALU.add))
            r(V.tensor_tensor(stat[:, 6, :], top[0], top[1], ALU.add))
            after_d()
            V.scalar_tensor_tensor(a_dt[:, :, :], dt_sb[:, :, :], -1.0,
                                   a_exp[:, :].unsqueeze(1).to_broadcast([P, TILES, HEADS]),
                                   ALU.mult, ALU.mult).then_inc(a_dt_ready, 1)
            after_r()
            r(V.tensor_scalar(stat[:, 6, :], stat[:, 6, :], 1e-9, None, ALU.max))
            after_r()
            r(V.reciprocal(stat[:, 7, :], stat[:, 6, :]))
            after_r()
            for k in range(CHOICES):
                V.tensor_tensor(rec[:, k, :, DM], top[k], stat[:, 7, :], ALU.mult).then_inc(gates_ready, 1)

            dve.wait_ge(place_psum, 1)
            places = bank[2][:, 0:P].rearrange("p (q e) -> p q e", e=EXPERTS)
            link(V.tensor_scalar(place[:, 0, :, :], places, float(CAP), DROPPED, ALU.is_ge, ALU.mult))
            link(V.tensor_tensor(place[:, 1, :, :], places, place[:, 0, :, :], ALU.add))
            link(V.tensor_tensor(place[:, 2, :, :], place[:, 1, :, :], slot0[:, :, :], ALU.add))
            link(V.tensor_tensor(place[:, 0, :, :], place[:, 2, :, :], hot[:, :, :], ALU.mult))
            link(V.tensor_reduce(slot_f[:, :], place[:, 0, :, :], AX_X, ALU.add))
            V.tensor_copy(slot_i[:, :], slot_f[:, :]).then_inc(slots_known, 1)

            def dve_slots(e, pair, u):
                dve.wait_ge(slots_t_psum, e + 1)
                V.tensor_copy(slots_t[:, u, :, :], bank[TRANSPOSED][:, :].rearrange("p (k s) -> p k s", k=KD)
                              ).then_inc(slots_t_ready, 1)
                dve.wait_ge(slots_loaded[u], (pair + 1) * 16)
                dve.wait_ge(eo_free, e + 1)
                V.tensor_copy(gate[:, u, :], slots[:, u, :, DM])
                V.tensor_scalar(row_t[:, :], slots[:, u, :, DM + 1], 0.0, DROPPED, ALU.is_equal, ALU.mult
                                ).then_inc(row_step, 1)
                dve.wait_ge(row_step, e + 1)
                V.scalar_tensor_tensor(row_i[:, u, :], slots[:, u, :, DM + 1], -1.0, row_t[:, :],
                                       ALU.add, ALU.add).then_inc(slot_info, 1)

            for j0 in range(0, len(XBC), 2):
                if j0 == DECAY_AT:
                    dve.wait_ge(decay_ready, 1)
                    V.tensor_tensor(decay[:, :, :], decay[:, :, :], dt_sb[:, :, :], ALU.mult).then_inc(decay_used, 1)
                for d in range(1, TAPS):
                    for j in (j0, j0 + 1):
                        i, m, n = XBC[j]
                        src = bank[PROJ_BANKS[i % NPB]][:, :].rearrange("p (b l) -> p b l", l=SEQ)
                        acc = conv[:, j % 4, :].rearrange("p (b l) -> p b l", l=SEQ)
                        if d == 1:
                            dve.wait_ge(tap_ready, j + 1)
                        else:
                            dve.wait_ge(conv_steps, 2 * (d - 2) + 2 * j0 + j - j0 + 1)
                        ins = V.scalar_tensor_tensor(acc[:, :, d:], src[:, :, 0:SEQ - d], tap(m, TAPS - 1 - d),
                                                     acc[:, :, d:], ALU.mult, ALU.add)
                        ins.then_inc(conv_steps if d < TAPS - 1 else conv_ready, 1)

            dve.sem_inc(eo_free, 2)
            dve_slots(0, 0, 0)
            dve.wait_ge(conv_read, len(XBC))
            dve.wait_ge(z_ready, HT * SPANS)

            def dve_step(n, pair, u, first=False, last=False):
                now = bass.ds(n * P, P)
                if not first:
                    sum_squares(n - 1)
                x_tok = bank[TRANSPOSED][:, :].rearrange("p (h l) -> p h l", h=HEADS)

                def per_step(a):
                    return a[:, bass.ds(n, 1), :].rearrange("p a h -> p (a h)").unsqueeze(2).to_broadcast([P, HEADS, P])

                dve.wait_ge(xt_psum, n + 1)
                V.tensor_tensor(xs[:, :, :], x_tok, per_step(dt_sb), ALU.mult).then_inc(xs_ready, 1)
                if u == 0:
                    V.tensor_tensor(xd[:, :, :], x_tok, per_step(decay), ALU.mult).then_inc(xd_ready, 1)
                dve.wait_ge(cb_psum, n + 1)
                V.tensor_tensor(cb[:, :], bank[CB_THEN_Y][:, 0:P], upto[:, :], ALU.mult).then_inc(cb_ready, 1)
                dve.wait_ge(cb_ready, n + 1)
                dve.wait_ge(seg_ready, n + 1)
                V.tensor_tensor(mix[:, :, :], mix[:, :, :], cb[:, :].unsqueeze(1).to_broadcast([P, HEADS, P]),
                                ALU.mult).then_inc(mix_ready, 1)
                if u == 1:
                    dve.wait_ge(cexp_ready, pair + 1)
                    V.tensor_tensor(c_dec[:, :, :], c_dec[:, :, :],
                                    c_low[:, now].unsqueeze(1).to_broadcast([STATE, HEADS, P]), ALU.mult
                                    ).then_inc(cdec_ready, 1)
                if not last:
                    dve_slots(n + 1, pair + u, 1 - u)
                for h in range(CH):
                    if last and h == CH - 1:
                        dve_gated(n, now)
                    dve.wait_ge(fc2_psum, n * CH + h + 1)
                    V.tensor_tensor(eo[:, u, h, :], bank[FC2_BANKS[h]][:, 0:DM], b2[:, u, :], ALU.add
                                    ).then_inc(fc2_read, 1)
                    dve.wait_ge(fc2_read, CH + n * CH + h + 1)
                    V.tensor_scalar(eo[:, u, h, :], eo[:, u, h, :], gate[:, u, h:h + 1], None, ALU.mult
                                    ).then_inc(eo_ready, 1)
                if not last:
                    dve_gated(n, now)

            def dve_gated(n, now):
                dve.wait_ge(y_psum, n + 1)
                for h in range(HT):
                    V.scalar_tensor_tensor(g[:, h, :], xc[:, h, now], d_skip(h), bank[CB_THEN_Y][:, h * P:(h + 1) * P],
                                           ALU.mult, ALU.add).then_inc(y_read, 1)
                dve.wait_ge(y_read, n * HT + HT)
                V.tensor_tensor(g[:, :, :], g[:, :, :], zs[:, :, now], ALU.mult).then_inc(g_ready, 1)

            def sum_squares(n):
                dve.wait_ge(gsq_ready, n + 1)
                V.tensor_reduce(gsum[:, :], gsq[:, :, :].rearrange("p h l -> p l h"), AX_X, ALU.add
                                ).then_inc(gsum_ready, 1)

            dve.wait_ge(bias_loaded[0], 32)
            dve.wait_ge(bias_loaded[1], 32)
            dve_step(0, 0, 0, first=True)
            with dve.Fori(0, STEPS // 2 - 1) as i:
                for u in (1, 0):
                    dve.wait_ge(bias_loaded[u], (i + 2 - u) * 32)
                    dve_step(i * 2 + 2 - u, i + 1 - u, u)
            dve.wait_ge(bias_loaded[1], STEPS // 2 * 32)
            dve_step(STEPS - 1, STEPS // 2 - 1, 1, last=True)
            sum_squares(STEPS - 1)

            dve.wait_ge(s_ready, TILES)
            ms, y_, t_ = rms[:, 0, :], rms[:, 1, :], rms[:, 2, :]
            link(V.tensor_scalar(ms, s_out[:, :, DM], 1.0 / DI, EPS, ALU.mult, ALU.add))
            link(V.tensor_scalar(y_.bitcast(U32), ms.bitcast(U32), 1, None, ALU.logical_shift_right))
            link(V.tensor_scalar(y_.bitcast(I32), y_.bitcast(I32), -1.0, float(0x5F3759DF), ALU.mult, ALU.add))
            for _ in range(3):
                link(V.tensor_tensor(t_, y_, y_, ALU.mult))
                link(V.scalar_tensor_tensor(t_, t_, -0.5, ms, ALU.mult, ALU.mult))
                link(V.scalar_tensor_tensor(y_, t_, 1.5, y_, ALU.add, ALU.mult))

            dve.wait_ge(dve_steps, chained[0])
            for i in range(4):
                t = slice(2 * i, 2 * i + 2)
                res = moe[:, 0, t, :]
                dve.wait_ge(moe_silu, i + 1)
                for j in range(2):
                    step(V.scalar_tensor_tensor(res[:, j, :], s_out[:, 2 * i + j, 0:DM], rms[:, 1, 2 * i + j:2 * i + j + 1],
                                                moe[:, 1, 2 * i + j, :], ALU.mult, ALU.mult))
                dve.wait_ge(dve_steps, chained[0])
                V.tensor_tensor(res, res, x_sb[:, t, :], ALU.add).then_inc(out_ready, 1)

        @block.tensor
        def _(pe):
            T = nc.tensor

            pe.wait_ge(zeros_ready, 1)
            for _ in range(WARM_UP):
                T.matmul(bank[7][:, 0:P], zeros[:, 0:P], zeros[:, 0:P], start=True, stop=True)

            pe.wait_ge(masks_ready, 8)
            pe.wait_ge(small_loaded, 48)

            def small_products(t):
                pe.wait_ge(xn_t_ready, t + 1)
                for k in range(KD):
                    last = T.matmul(bank[3][:, t * NSMALL:(t + 1) * NSMALL], xn_t[:, k, t * P:(t + 1) * P],
                                    wsmall[:, k, :], start=(k == 0), stop=(k == KD - 1))
                return last

            for t in range(TILES):
                pe.wait_ge(xn_ready[t % 2], t // 2 + 1)
                if t >= 2:
                    pe.wait_ge(xn_t_ready, t - 1)
                for k in range(KD):
                    last = T.transpose(bank[t % 2][:, k * P:(k + 1) * P], rec[:, 0, t, k * P:(k + 1) * P], ident[:, :])
                last.then_inc(xn_t_psum, 1)
                if t >= 2:
                    small_products(t - 2)
            small_products(TILES - 2)
            small_products(TILES - 1).then_inc(small_psum, 1)

            def place_products():
                pe.wait_ge(hot_ready, 1)
                q = CHOICES * TILES
                rows = hot[:, :, :]
                T.matmul(bank[2][:, 0:q * EXPERTS], before16[:, :], rows.rearrange("p q e -> p (q e)"),
                         start=True, stop=False)
                for n in range(q - 1):
                    dst = bank[2][:, (n + 1) * EXPERTS:q * EXPERTS].rearrange("p (q e) -> p q e", e=EXPERTS)
                    last = T.matmul(dst, ones16[:, :],
                                    hot[:, n, :].unsqueeze(1).to_broadcast([P, q - 1 - n, EXPERTS]),
                                    start=False, stop=(n == q - 2))
                last.then_inc(place_psum, 1)

            def slots_transposed(e, pair, u):
                pe.wait_ge(slots_loaded[u], (pair + 1) * 16)
                for k in range(KD):
                    for h in range(CH):
                        last = T.transpose(bank[TRANSPOSED][:, k * CAP + h * P:k * CAP + (h + 1) * P],
                                           slots[:, u, h, k * P:(k + 1) * P], ident[:, :])
                last.then_inc(slots_t_psum, 1)

            def projected_read(i):
                kind, m, n = PROJ[i]
                if kind == "z":
                    pe.wait_ge(z_ready, Z.index((kind, m, n)) + 1)
                else:
                    pe.wait_ge(conv_ready, convolved(m, n))

            for i, (kind, m, n) in enumerate(PROJ):
                pe.wait_ge(win_loaded[0 if kind == "z" else 1], 16)
                if i == PLACES_AT:
                    place_products()
                if i == PLACES_AT + 4:
                    pe.wait_ge(a_dt_ready, 1)
                    pe.wait_ge(slots_known, 1)
                    T.matmul(bank[2][:, 0:TILES * HEADS], later[:, :], a_dt[:, :, :].rearrange("p t h -> p (t h)"),
                             start=True, stop=True).then_inc(decay_psum, 1)
                if i == 0:
                    pe.wait_ge(xn_t_ready, TILES)
                if i >= NPB:
                    projected_read(i - NPB)
                c = col0(kind, m)
                for k in range(KD):
                    last = T.matmul(bank[PROJ_BANKS[i % NPB]][:, :], win[:, k, c:c + P], xn_t[:, k, n * SPAN:(n + 1) * SPAN],
                                    start=(k == 0), stop=(k == KD - 1))
                last.then_inc(proj_psum, 1)

            def fc1(n, pair, u, tiles=range(FT)):
                pe.wait_ge(slots_t_ready, n + 1)
                pe.wait_ge(w_loaded[0][u], (pair + 1) * 16)
                for f in tiles:
                    pe.wait_ge(hid_ready, n * FT + f + 1)
                    for k in range(KD):
                        last = T.matmul(bank[FC1_BANKS[f % NB1]][:, 0:CAP], w1[:, u, k, f * P:(f + 1) * P],
                                        slots_t[:, u, k, :], start=(k == 0), stop=(k == KD - 1))
                    last.then_inc(fc1_psum, 1)

            def fc2(n, u, h):
                pe.wait_ge(fc2_read, n * CH + h + 1)
                for f in range(FT):
                    if h == 0:
                        pe.wait_ge(hid_ready, n * FT + NB1 + f + 1)
                    last = T.matmul(bank[FC2_BANKS[h]][:, 0:DM], hid[:, f, h * P:(h + 1) * P], w2[:, u, f, :],
                                    start=(f == 0), stop=(f == FT - 1))
                last.then_inc(fc2_psum, 1)

            def out_proj(n):
                dst = bank[OUT_THEN_STATE]
                pe.wait_ge(g_ready, n + 1)
                for h in range(HT):
                    T.matmul(dst[:, 0:DM], g[:, h, :], wout[:, h, :], start=(h == 0), stop=(h == HT - 1))
                pe.wait_ge(gsum_ready, n + 1)
                T.matmul(dst[:, DM:DM + 1], gsum[:, :], ones[:, 0:1], start=True, stop=True).then_inc(s_psum, 1)

            def chunk_inputs(n, pair, u, first):
                now = bass.ds(n * P, P)
                pe.wait_ge(chunk_staged, n * 2 + 2)
                pe.wait_ge(slots_t_ready, n + 1)
                for h in range(HT):
                    last = T.transpose(bank[TRANSPOSED][:, h * P:(h + 1) * P], x_chunk[:, h, :], ident[:, :])
                last.then_inc(xt_psum, 1)
                if not first:
                    pe.wait_ge(y_read, n * HT)
                T.matmul(bank[CB_THEN_Y][:, 0:P], bc_chunk[0:STATE, :], c_low[:, now],
                         start=True, stop=True).then_inc(cb_psum, 1)
                pe.wait_ge(a_upto_ready, n + 1)
                if not first:
                    pe.wait_ge(seg_ready, n)
                steps = a_upto[:, :, :].rearrange("p h l -> p (h l)")
                T.matmul(bank[SEG][:, :], later[:, :], steps, start=True, stop=True).then_inc(seg_psum, 1)
                if not first:
                    pe.wait_ge(s_ready, n)
                if u == 0:
                    T.transpose(bank[OUT_THEN_STATE][:, 0:P], bc_chunk[:, :], ident[:, :]).then_inc(last_in_psum, 1)
                else:
                    T.matmul(bank[OUT_THEN_STATE][0:STATE, :], ones[:, :], steps,
                             start=True, stop=True).then_inc(last_in_psum, 1)

            def chunk_state(pair):
                pe.wait_ge(xd_ready, pair + 1)
                pe.wait_ge(b_tok_ready, pair + 1)
                T.matmul(bank[OUT_THEN_STATE][0:STATE, :], b_tok[:, :], xd[:, :, :].rearrange("p h l -> p (h l)"),
                         start=True, stop=True).then_inc(state_psum, 1)

            def chunk_y(n, pair, u):
                pe.wait_ge(xs_ready, n + 1)
                pe.wait_ge(mix_ready, n + 1)
                if u == 1:
                    pe.wait_ge(state_ready, pair + 1)
                    pe.wait_ge(cdec_ready, pair + 1)
                for h in range(HEADS):
                    dst = bank[CB_THEN_Y][:, h * P:(h + 1) * P]
                    last = T.matmul(dst, xs[:, h, :], mix[:, h, :], start=True, stop=(u == 0))
                    if u == 1:
                        last = T.matmul(dst, state[:, h, :], c_dec[:, h, :], start=False, stop=True)
                last.then_inc(y_psum, 1)

            def pe_step(n, pair, u, first=False, last=False):
                fc1(n, pair, u, range(NB1) if first else range(FT))
                if first:
                    pe.wait_ge(conv_ready, len(XBC))
                    pe.wait_ge(z_ready, HT * SPANS)
                    for m in range(SPANS):
                        pe.wait_ge(c_moved[m], 16)
                    pe.wait_ge(wout_scaled, HT)
                else:
                    out_proj(n - 1)
                chunk_inputs(n, pair, u, first)
                if first:
                    fc1(n, pair, u, range(NB1, FT))
                pe.wait_ge(xs_ready, n + 1)
                if u == 0:
                    pe.wait_ge(xd_ready, pair + 1)
                if not last:
                    slots_transposed(n + 1, pair + u, 1 - u)
                pe.wait_ge(w_loaded[1][u], (pair + 1) * 16)
                fc2(n, u, 0)
                if u == 0:
                    chunk_state(pair)
                if last:
                    chunk_y(n, pair, u)
                fc2(n, u, 1)
                if u == 1:
                    pe.wait_ge(cexp_ready, pair + 1)
                if not last:
                    chunk_y(n, pair, u)

            for i in range(2):
                projected_read(len(PROJ) - NPB + i)
            pe.wait_ge(decay_ready, 1)
            slots_transposed(0, 0, 0)
            pe.sem_inc(hid_ready, NB1)
            pe.sem_inc(fc2_read, CH)
            pe_step(0, 0, 0, first=True)
            with pe.Fori(0, STEPS // 2 - 1) as i:
                pe_step(i * 2 + 1, i, 1)
                pe_step(i * 2 + 2, i + 1, 0)
            pe_step(STEPS - 1, STEPS // 2 - 1, 1, last=True)
            out_proj(STEPS - 1)


def kernel(**inputs):
    import numpy as np
    import concourse.bacc as bacc
    from concourse.bass_utils import run_bass_kernel_spmd

    a = {k.split("_", 2)[2]: np.asarray(v) for k, v in inputs.items()}
    di, heads, taps = a["W_out"].shape[1], a["A_log"].shape[0], a["W_conv"].shape[2]
    w_in_t = np.ascontiguousarray(a["W_in"].T)
    small0 = w_in_t.shape[1] - heads
    ctiles = a["W_conv"].shape[0] // P
    channels = np.concatenate([
        a["W_conv"].reshape(ctiles, P, taps).transpose(1, 0, 2).reshape(P, ctiles * taps),
        a["b_conv"].reshape(ctiles, P).T, a["norm_w"].reshape(di // P, P).T], axis=1)
    e, hidden = a["fc1_b"].shape
    arrays = {
        "x": a["u"].reshape(-1, a["u"].shape[-1]),
        "w_in_t": w_in_t,
        "w_small": np.concatenate([w_in_t[:, small0:], a["wg"]], axis=1),
        "head_params": np.concatenate([a["dt_bias"], a["A_log"], a["D"]])[None],
        "channel_params": channels,
        "w_out_t": a["W_out"].T,
        "fc1_w": a["fc1_w"],
        "fc1_b": a["fc1_b"].reshape(e, hidden // P, P).transpose(0, 2, 1),
        "fc2_w": a["fc2_w"],
        "fc2_b": a["fc2_b"],
    }
    arrays = {k: np.ascontiguousarray(v) for k, v in arrays.items()}
    nc = bacc.Bacc("TRN2", target_bir_lowering=False, num_devices=1)
    args = [nc.dram_tensor(k, v.shape, mybir.dt.from_np(v.dtype), kind="ExternalInput").ap() for k, v in arrays.items()]
    args.append(nc.dram_tensor("out", arrays["x"].shape, F32, kind="ExternalOutput").ap())
    layer(nc, *args)
    r = run_bass_kernel_spmd(nc, [arrays], core_ids=[0])
    return r.results[0]["out"].reshape(a["u"].shape)
```

```python
from contextlib import ExitStack

import concourse.bass as bass
from concourse import mybir

F32 = mybir.dt.float32
BF16 = mybir.dt.bfloat16
I32 = mybir.dt.int32
U32 = mybir.dt.uint32
F16 = mybir.dt.float16
ALU = mybir.AluOpType
ACT = mybir.ActivationFunctionType
AX_X = mybir.AxisListType.X

P = 128
TAPS = 4
EPS = 1e-5
XN_SCALE = 1024.0
EXP1 = float(1 << 23)
DROPPED = float(1 << 20)


def layer(nc, x, w_in_t, w_small, head_params, channel_params, w_out_t,
          fc1_w, fc1_b, fc2_w, fc2_b, out):
    TOKENS, DM = x.shape
    KD = DM // P
    TILES = TOKENS // P
    HEADS = head_params.shape[1] // 3
    DI = w_out_t.shape[0]
    HT = DI // P
    STATE = (w_in_t.shape[1] - 2 * DI - HEADS) // 2
    EXPERTS, _, HIDDEN = fc1_w.shape
    FT = HIDDEN // P
    CHOICES = 2
    CAP = CHOICES * TOKENS // EXPERTS
    SLOTS = EXPERTS * CAP
    CH = CAP // P
    REC = DM + 2
    PARTS = 2
    FS = 4
    SPAN = 512
    SPANS = TOKENS // SPAN
    TPS = SPAN // P
    SEQ = 256
    NSMALL = HEADS + EXPERTS
    CTILES = HT + 1
    assert HT == HEADS and STATE == 64 and CH == 2 and KD == 2

    slots_dram = nc.dram_tensor("expert_slots", [SLOTS, REC], F32).ap()
    moe_dram = nc.dram_tensor("moe_rows", [TOKENS, DM], F32).ap()

    with ExitStack() as ctx:
        def sb(name, shape, dt=F32):
            return ctx.enter_context(nc.sbuf_tensor(name, shape, dt))

        def sem(name):
            return ctx.enter_context(nc.semaphore(name))

        bank = [ctx.enter_context(nc.psum_tensor(f"bank{i}", [P, 512], F32)) for i in range(8)]

        x_sb = sb("x_sb", [P, TILES, DM])
        rec = sb("rec", [P, CHOICES, TILES, REC])
        ident16 = sb("ident16", [P, P], F16)
        xn_t = sb("xn_t", [P, KD, TOKENS])
        win = sb("win", [P, KD, w_in_t.shape[1]])
        wsmall = sb("wsmall", [P, KD, NSMALL])
        heads = sb("heads", [P, 3 * HEADS])
        chan = sb("chan", [P, CTILES * TAPS + CTILES + HT])
        wout = sb("wout", [P, HT, DM])
        zs = sb("zs", [P, HT, TOKENS])
        xc = sb("xc", [P, HT, TOKENS])
        bc = sb("bc", [P, TOKENS])
        c_low = sb("c_low", [STATE, TOKENS])
        conv = sb("conv", [P, 4, SPAN])
        ident = sb("ident", [P, P])
        later = sb("later", [P, P])
        upto = sb("upto", [P, P])
        ones = sb("ones", [P, P])
        later16 = sb("later16", [P, P], BF16)
        upto16 = sb("upto16", [P, P], BF16)
        before16 = sb("before16", [P, P], BF16)
        ones16 = sb("ones16", [P, P], BF16)
        zeros = sb("zeros", [P, 4 * REC])
        prefer = sb("prefer", [P, EXPERTS])
        slot0 = sb("slot0", [P, CHOICES * TILES, EXPERTS])
        bn = sb("bn", [P, TILES, 6])
        mv = sb("mv", [P, TILES, 2])
        std = sb("std", [P, TILES])
        rstd = sb("rstd", [P, TILES])
        shift = sb("shift", [P, TILES])
        lg = sb("lg", [P, TILES, EXPERTS])
        ex = sb("ex", [P, TILES, EXPERTS])
        sc = sb("sc", [P, CHOICES, TILES, EXPERTS])
        key = sb("key", [P, TILES, EXPERTS])
        stat = sb("stat", [P, 10, TILES])
        hot = sb("hot", [P, CHOICES * TILES, EXPERTS], BF16)
        place = sb("place", [P, 3, CHOICES * TILES, EXPERTS])
        slot_f = sb("slot_f", [P, CHOICES * TILES])
        slot_i = sb("slot_i", [P, CHOICES * TILES], I32)
        dtw = sb("dtw", [P, 10, TILES, HEADS])
        a_exp = sb("a_exp", [P, HEADS])
        a_dt = sb("a_dt", [P, TILES, HEADS])
        dt_sb = sb("dt_sb", [P, TILES, HEADS])
        decay = sb("decay", [P, TILES, HEADS])
        a_rest = sb("a_rest", [P, 2, TILES, HEADS])
        a_parts = sb("a_parts", [P, 3, TILES, HEADS], BF16)
        a_upto = sb("a_upto", [P, 3, HEADS, P], BF16)
        x_chunk = sb("x_chunk", [P, HT, P])
        bc_chunk = sb("bc_chunk", [P, P])
        mix = sb("mix", [P, HEADS, P])
        cb = sb("cb", [P, P])
        xs = sb("xs", [P, HEADS, P])
        xd = sb("xd", [P, HEADS, P])
        b_tok = sb("b_tok", [P, STATE])
        state = sb("state", [STATE, HEADS, P])
        c_dec = sb("c_dec", [STATE, HEADS, P])
        g = sb("g", [P, HT, P])
        gsq = sb("gsq", [P, HT, P])
        gsum = sb("gsum", [P, P])
        s_out = sb("s_out", [P, TILES, DM + 1])
        rms = sb("rms", [P, 4, TILES])
        w1 = sb("w1", [P, 2, KD, HIDDEN])
        w2 = sb("w2", [P, 2, FT, DM])
        b1 = sb("b1", [P, 2, FT])
        b2 = sb("b2", [P, 2, DM])
        slots = sb("slots", [P, 2, CH, REC])
        slots_t = sb("slots_t", [P, 2, PARTS, KD, CAP], F16)
        hid = sb("hid", [P, FT, CAP])
        w1s = sb("w1s", [P, 2, PARTS, KD, HIDDEN], F16)
        squares = sb("squares", [P, 3])
        nothing = sb("nothing", [P, FT + 1])
        scales = sb("scales", [P, 2, 13])
        eo = sb("eo", [P, 2, CH, DM])
        gate = sb("gate", [P, 2, CH])
        row_t = sb("row_t", [P, CH])
        row_i = sb("row_i", [P, 2, CH], I32)
        moe = w1[:, :, :, :].rearrange("p u k f -> p u (k f)").rearrange("p u (t c) -> p u t c", c=DM)

        xn = hid[:, :, :].rearrange("p f s -> p (f s)").rearrange("p (t c) -> p t c", c=DM)
        halves = [[rec[:, 0, t, 0:DM].bitcast(F16)[:, part * DM:(part + 1) * DM] for part in range(PARTS)]
                  for t in range(TILES)]

        hids = xn_t[:, :, :].rearrange("p k t -> p (k t)")[:, 0:FS * CAP].bitcast(F16).rearrange(
            "p (a f s) -> p a f s", a=PARTS, f=FS)
        w2s = rec[:, :, :, :].rearrange("p k t r -> p (k t r)")[:, 0:2 * FS * DM].bitcast(F16).rearrange(
            "p (u a f c) -> p u a f c", u=2, a=PARTS, f=FS)

        def w_whole(j, u):
            return (w2[:, u, 0:FS, :] if j else w1[:, u, :, :]).rearrange("p a b -> p (a b)")

        def w_part(j, u, part):
            return (w2s if j else w1s)[:, u, part, :, :].rearrange("p a b -> p (a b)")

        def scale(u, name, n=1):
            i = ["exponents", "exponent2", "w1", "w2", "fc1_back", "hidden", "hidden_back", "w2_back",
                 "hidden_w2", "fc2_back", "sums", "sum2", "bias_sum"].index(name)
            return scales[:, u, i:i + n]

        x_loaded = [sem(f"x_loaded{i}") for i in range(2)]
        small_loaded = sem("small_loaded")
        win_loaded = [sem(f"win_loaded{i}") for i in range(2)]
        wout_loaded = sem("wout_loaded")
        zeros_ready = sem("zeros_ready")
        dram_cleared = sem("dram_cleared")
        masks_ready = sem("masks_ready")
        pool_steps = sem("pool_steps")
        router_steps = sem("router_steps")
        dt_steps = sem("dt_steps")
        dve_steps = sem("dve_steps")
        var_ready = sem("var_ready")
        std_ready = sem("std_ready")
        xn_ready = [sem(f"xn_ready{i}") for i in range(2)]
        shift_ready = sem("shift_ready")
        rec_numbered = sem("rec_numbered")
        high_ready = sem("high_ready")
        low_ready = sem("low_ready")
        rec_copied = sem("rec_copied")
        squares_ready = sem("squares_ready")
        squares_psum = sem("squares_psum")
        exponent_ready = sem("exponent_ready")
        scale_ready = sem("scale_ready")
        sums_ready = sem("sums_ready")
        backs_ready = sem("backs_ready")
        fc2_scales_ready = sem("fc2_scales_ready")
        w_high = [sem(f"w{j}_high") for j in (1, 2)]
        w_split = [sem(f"w{j}_split") for j in (1, 2)]
        hid_high = sem("hid_high")
        hid_split = sem("hid_split")
        xn_t_psum = sem("xn_t_psum")
        xn_t_ready = sem("xn_t_ready")
        small_psum = sem("small_psum")
        exp_in_ready = sem("exp_in_ready")
        exp_out_ready = sem("exp_out_ready")
        hot_ready = sem("hot_ready")
        place_psum = sem("place_psum")
        slots_known = sem("slots_known")
        gates_ready = sem("gates_ready")
        scattered = [sem(f"scattered{i}") for i in range(4)]
        proj_psum = sem("proj_psum")
        tap_ready = sem("tap_ready")
        conv_steps = sem("conv_steps")
        conv_ready = sem("conv_ready")
        conv_read = sem("conv_read")
        z_ready = sem("z_ready")
        c_moved = [sem(f"c_moved{i}") for i in range(SPANS)]
        a_dt_ready = sem("a_dt_ready")
        decay_psum = sem("decay_psum")
        decay_ready = sem("decay_ready")
        decay_used = sem("decay_used")
        a_split = sem("a_split")
        a_upto_ready = sem("a_upto_ready")
        chunk_staged = sem("chunk_staged")
        wout_scaled = sem("wout_scaled")
        xt_psum = sem("xt_psum")
        xs_ready = sem("xs_ready")
        xd_ready = sem("xd_ready")
        cb_psum = sem("cb_psum")
        cb_ready = sem("cb_ready")
        seg_psum = sem("seg_psum")
        seg_ready = sem("seg_ready")
        mix_ready = sem("mix_ready")
        last_in_psum = sem("last_in_psum")
        b_tok_ready = sem("b_tok_ready")
        cexp_ready = sem("cexp_ready")
        cdec_ready = sem("cdec_ready")
        state_psum = sem("state_psum")
        state_ready = sem("state_ready")
        y_psum = sem("y_psum")
        y_read = sem("y_read")
        g_ready = sem("g_ready")
        gsq_ready = sem("gsq_ready")
        gsum_ready = sem("gsum_ready")
        s_psum = sem("s_psum")
        s_ready = sem("s_ready")
        w_loaded = [[sem(f"w{j}_loaded{u}") for u in range(2)] for j in (1, 2)]
        bias_loaded = [sem(f"bias_loaded{u}") for u in range(2)]
        slots_loaded = [sem(f"slots_loaded{u}") for u in range(2)]
        slots_t_psum = sem("slots_t_psum")
        slots_t_ready = sem("slots_t_ready")
        fc1_psum = sem("fc1_psum")
        hid_ready = sem("hid_ready")
        fc2_psum = sem("fc2_psum")
        fc2_read = sem("fc2_read")
        row_step = sem("row_step")
        slot_info = sem("slot_info")
        eo_ready = sem("eo_ready")
        eo_free = sem("eo_free")
        rows_scattered = [[sem(f"rows_scattered{u}{h}") for h in range(CH)] for u in range(2)]
        moe_loaded = [sem(f"moe_loaded{i}") for i in range(4)]
        moe_silu = sem("moe_silu")
        product_ready = sem("product_ready")
        out_ready = [sem(f"out_ready{i}") for i in range(2)]
        stored = sem("stored")

        x_v = x.rearrange("(t p) d -> p t d", p=P)
        out_v = out.rearrange("(t p) d -> p t d", p=P)
        moe_v = moe_dram.rearrange("(t p) d -> p t d", p=P)
        slots_v = slots_dram.rearrange("(e h p) r -> e p h r", p=P, h=CH)
        win_v = w_in_t.rearrange("(k p) c -> p k c", p=P)
        w1_v = fc1_w.rearrange("e (k p) f -> e p k f", p=P)
        w2_v = fc2_w.rearrange("e (f p) d -> e p f d", p=P)
        HALF = TILES // 2
        STEPS = EXPERTS
        assert STEPS == TILES
        dt_bias = heads[:, 0:HEADS]
        a_log = heads[:, HEADS:2 * HEADS]

        def d_skip(h):
            return heads[:, 2 * HEADS + h:2 * HEADS + h + 1]

        def tap(c, j):
            return chan[:, c * TAPS + j:c * TAPS + j + 1]

        def conv_bias(c):
            return chan[:, CTILES * TAPS + c:CTILES * TAPS + c + 1]

        def norm_w(h):
            return chan[:, CTILES * TAPS + CTILES + h:CTILES * TAPS + CTILES + h + 1]

        Z = [("z", m, n) for n in range(SPANS) for m in range(HT)]
        X = [("xbc", m, n) for n in range(SPANS) for m in [HT] + list(range(HT))]
        PROJ = Z[0:4] + X[0:4] + Z[4:5] + X[4:8] + Z[5:7] + X[8:10] + Z[7:]
        PROJ_BANKS = [5, 0, 1, 6, 7, 4]
        NPB = len(PROJ_BANKS)
        WARM_UP = 14
        SQUARES_AT = 8
        DECAY_AT = 6
        PLACES_AT = 3
        XBC = [(i, m, n) for i, (kind, m, n) in enumerate(PROJ) if kind == "xbc"]
        TRANSPOSED, FC1_BANKS, FC2_BANKS, SEG, CB_THEN_Y, OUT_THEN_STATE = 0, [1, 2, 3, 4], [3, 4], 5, 6, 7
        NB1 = len(FC1_BANKS)
        FIRST_SUM = bank[3][:, TILES * NSMALL:TILES * NSMALL + 1]
        PRODUCTS = [(0, 0), (0, 1), (1, 0)]

        def col0(kind, m):
            return m * P if kind == "z" else DI + m * P

        def convolved(c, n):
            return next(j for j, (_, m, nn) in enumerate(XBC) if (m, nn) == (c, n)) + 1

        block = ctx.enter_context(nc.Block())

        @block.sync
        def _(sp):
            for i in range(2):
                half = slice(i * HALF, (i + 1) * HALF)
                sp.dma_start(x_sb[:, half, :], x_v[:, half, :]).then_inc(x_loaded[i], 16)
            for n in range(2):
                c = slice(n * DI, DI if n == 0 else w_in_t.shape[1])
                sp.dma_start(win[:, :, c], win_v[:, :, c]).then_inc(win_loaded[n], 16)
            def load_w1(e, u):
                sp.dma_start(w1[:, u, :, :], w1_v[e:e + 1].rearrange("e p k f -> (e p) k f")
                             ).then_inc(w_loaded[0][u], 16)

            def load_biases(e, u):
                sp.dma_start(b1[:, u, :], fc1_b[e:e + 1].rearrange("e p f -> (e p) f")
                             ).then_inc(bias_loaded[u], 16)
                sp.dma_start(b2[:, u, :], fc2_b[e:e + 1].to_broadcast([P, DM])
                             ).then_inc(bias_loaded[u], 16)

            def load_w2(e, u):
                sp.dma_start(w2[:, u, :, :], w2_v[e:e + 1].rearrange("e p f d -> (e p) f d")
                             ).then_inc(w_loaded[1][u], 16)

            load_w1(0, 0)
            load_biases(0, 0)
            load_w2(0, 0)
            sp.wait_ge(zeros_ready, 1)
            for i in range(SLOTS // (4 * P)):
                dst = slots_dram[i * 4 * P:(i + 1) * 4 * P, :].rearrange("(p r) c -> p (r c)", p=P)
                sp.dma_start(dst, zeros[:, :]).then_inc(dram_cleared, 16)
            for i in range(TOKENS // (4 * P)):
                dst = moe_dram[i * 4 * P:(i + 1) * 4 * P, :].rearrange("(p r) c -> p (r c)", p=P)
                sp.dma_start(dst, zeros[:, 0:4 * DM]).then_inc(dram_cleared, 16)
            sp.dma_start(wout[:, :, :], w_out_t.rearrange("(h p) d -> p h d", p=P)).then_inc(wout_loaded, 16)

            def load_slots(e, u):
                sp.dma_start(slots[:, u, :, :], slots_v[e:e + 1].rearrange("e p h r -> (e p) h r")
                             ).then_inc(slots_loaded[u], 16)

            load_w1(1, 1)
            load_biases(1, 1)
            load_w2(1, 1)
            sp.wait_ge(low_ready, TILES)
            sp.dma_start(rec[:, 1, :, 0:DM], rec[:, 0, :, 0:DM]).then_inc(rec_copied, 16)
            for s in scattered:
                sp.wait_ge(s, 16 * CHOICES * TILES // 4)
            load_slots(0, 0)
            load_slots(1, 1)
            for e in range(STEPS - 2):
                sp.wait_ge(w_split[0], e + 1)
                load_w1(e + 2, e % 2)
                sp.wait_ge(slots_t_psum, e + 1)
                sp.wait_ge(slot_info, e + 1)
                load_slots(e + 2, e % 2)
                sp.wait_ge(fc2_psum, (e + 1) * CH)
                sp.wait_ge(fc2_read, CH + (e + 1) * CH)
                load_biases(e + 2, e % 2)
                load_w2(e + 2, e % 2)

            for u in range(2):
                for h in range(CH):
                    sp.wait_ge(rows_scattered[u][h], 16 * STEPS // 2)
            for i in range(4):
                t = slice(2 * i, 2 * i + 2)
                sp.dma_start(moe[:, 0, t, :], moe_v[:, t, :]).then_inc(moe_loaded[i], 16)
            for i in range(4):
                t = slice(2 * i, 2 * i + 2)
                sp.wait_ge(out_ready[i // 3], 1 if i == 3 else i + 1)
                sp.dma_start(out_v[:, t, :], moe[:, 0, t, :]).then_inc(stored, 16)
            sp.wait_ge(stored, 64)

        @block.gpsimd
        def _(pool):
            done = [0]

            def step(ins):
                done[0] += 1
                return ins.then_inc(pool_steps, 1)

            nc.gpsimd.memset(zeros[:, :], 0.0).then_inc(zeros_ready, 1)
            step(nc.gpsimd.memset(ident[:, :], 0.0))
            step(nc.gpsimd.memset(ident16[:, :], 0.0))
            step(nc.gpsimd.memset(later[:, :], 1.0))
            step(nc.gpsimd.memset(upto[:, :], 1.0))
            step(nc.gpsimd.memset(before16[:, :], 1.0))
            pool.wait_ge(pool_steps, 5)
            nc.gpsimd.affine_select(out=ident[:, :], in_=ident[:, :], compare_op=ALU.not_equal, fill=1.0,
                                    base=0, pattern=[[-1, P]], channel_multiplier=1).then_inc(masks_ready, 1)
            nc.gpsimd.affine_select(out=ident16[:, :], in_=ident16[:, :], compare_op=ALU.not_equal, fill=1.0,
                                    base=0, pattern=[[-1, P]], channel_multiplier=1).then_inc(masks_ready, 1)
            nc.gpsimd.affine_select(out=before16[:, :], in_=before16[:, :], compare_op=ALU.is_gt, fill=0.0,
                                    base=0, pattern=[[1, P]], channel_multiplier=-1).then_inc(masks_ready, 1)
            nc.gpsimd.memset(ones16[:, :], 1.0).then_inc(masks_ready, 1)
            nc.gpsimd.iota(prefer[:, :], pattern=[[-1, EXPERTS]], base=EXPERTS, channel_multiplier=0,
                           allow_small_or_imprecise_dtypes=True).then_inc(masks_ready, 1)
            nc.gpsimd.iota(slot0[:, :, :], pattern=[[0, CHOICES * TILES], [CAP, EXPERTS]], base=0,
                           channel_multiplier=0, allow_small_or_imprecise_dtypes=True).then_inc(masks_ready, 1)
            nc.gpsimd.affine_select(out=later[:, :], in_=later[:, :], compare_op=ALU.is_gt, fill=0.0,
                                    base=0, pattern=[[-1, P]], channel_multiplier=1).then_inc(masks_ready, 1)
            nc.gpsimd.affine_select(out=upto[:, :], in_=upto[:, :], compare_op=ALU.is_ge, fill=0.0,
                                    base=0, pattern=[[1, P]], channel_multiplier=-1).then_inc(masks_ready, 1)
            pool.wait_ge(masks_ready, 8)
            nc.gpsimd.tensor_copy(later16[:, :], later[:, :]).then_inc(masks_ready, 1)
            nc.gpsimd.tensor_copy(upto16[:, :], upto[:, :]).then_inc(masks_ready, 1)
            nc.gpsimd.memset(ones[:, :], 1.0).then_inc(masks_ready, 1)
            for k in range(CHOICES):
                nc.gpsimd.iota(rec[:, k, :, DM + 1], pattern=[[P, TILES]], base=1,
                               channel_multiplier=1, allow_small_or_imprecise_dtypes=True
                               ).then_inc(rec_numbered, 1)
            for t in range(TILES):
                pool.wait_ge(xn_ready[t % 2], t // 2 + 1)
                nc.gpsimd.tensor_scalar(halves[t][0], xn[:, t, :], XN_SCALE, None, ALU.mult).then_inc(high_ready, 1)
            pool.wait_ge(a_dt_ready, 1)
            pool.wait_ge(masks_ready, 11)
            rest = a_dt[:, :, :]
            for k in range(3):
                nc.gpsimd.tensor_copy(a_parts[:, k, :, :], rest).then_inc(a_split, 1)
                pool.wait_ge(a_split, 2 * k + 1)
                if k < 2:
                    nc.gpsimd.tensor_tensor(a_rest[:, k, :, :], rest, a_parts[:, k, :, :], ALU.subtract
                                            ).then_inc(a_split, 1)
                    pool.wait_ge(a_split, 2 * k + 2)
                    rest = a_rest[:, k, :, :]

            def stage_decays(n):
                for k in range(3):
                    nc.gpsimd.tensor_tensor(
                        a_upto[:, k, :, :], a_parts[:, k, n, :].unsqueeze(2).to_broadcast([P, HEADS, P]),
                        upto16[:, :].unsqueeze(1).to_broadcast([P, HEADS, P]), ALU.mult).then_inc(a_upto_ready, 1)

            stage_decays(0)
            pool.wait_ge(rec_numbered, CHOICES)
            pool.wait_ge(low_ready, TILES)
            pool.wait_ge(gates_ready, CHOICES)
            pool.wait_ge(slots_known, 1)
            pool.wait_ge(dram_cleared, 16 * (SLOTS + TOKENS) // (4 * P))
            for q in range(CHOICES * TILES):
                k, t = divmod(q, TILES)
                if q == TILES:
                    pool.wait_ge(rec_copied, 16)
                nc.gpsimd.indirect_dma_start(
                    out=slots_dram, out_offset=bass.IndirectOffsetOnAxis(ap=slot_i[:, q:q + 1].bitcast(U32), axis=0),
                    in_=rec[:, k, t, :], in_offset=None, bounds_check=SLOTS - 1, oob_is_err=False,
                ).then_inc(scattered[q % 4], 16)

            def stage(n):
                now = slice(n * P, (n + 1) * P)
                if n % TPS == 0:
                    pool.wait_ge(conv_read, (n // TPS + 1) * CTILES)
                if n >= 1:
                    pool.wait_ge(last_in_psum, n)
                nc.gpsimd.tensor_copy(x_chunk[:, :, :], xc[:, :, now]).then_inc(chunk_staged, 1)
                nc.gpsimd.tensor_copy(bc_chunk[:, :], bc[:, now]).then_inc(chunk_staged, 1)
                if n >= 1:
                    stage_decays(n)

            pool.wait_ge(wout_loaded, 16)
            pool.wait_ge(small_loaded, 48)
            for h in range(HT):
                nc.gpsimd.tensor_scalar(wout[:, h, :], wout[:, h, :], norm_w(h), None, ALU.mult
                                        ).then_inc(wout_scaled, 1)

            stage(0)
            for e in range(STEPS):
                if e + 1 < STEPS:
                    stage(e + 1)
                u = e % 2
                for h in range(CH):
                    pool.wait_ge(eo_ready, e * CH + h + 1)
                    nc.gpsimd.indirect_dma_start(
                        out=moe_dram,
                        out_offset=bass.IndirectOffsetOnAxis(ap=row_i[:, u, h:h + 1].bitcast(U32), axis=0),
                        in_=eo[:, u, h, :], in_offset=None, bounds_check=TOKENS - 1,
                        oob_is_err=False, compute_op=ALU.add).then_inc(rows_scattered[u][h], 16)
                for h in range(CH):
                    pool.wait_ge(rows_scattered[u][h], 16 * (e // 2 + 1))
                pool.sem_inc(eo_free, 1)

            for i in range(3):
                t = slice(2 * i, 2 * i + 2)
                pool.wait_ge(product_ready, i + 1)
                nc.gpsimd.tensor_tensor(moe[:, 0, t, :], moe[:, 0, t, :], x_sb[:, t, :], ALU.add
                                        ).then_inc(out_ready[0], 1)

        @block.scalar
        def _(act):
            act.dma_start(wsmall[:, :, :], w_small.rearrange("(k p) c -> p k c", p=P)).then_inc(small_loaded, 16)
            act.dma_start(heads[:, :], head_params[0:1, :].to_broadcast([P, 3 * HEADS])).then_inc(small_loaded, 16)
            act.dma_start(chan[:, :], channel_params).then_inc(small_loaded, 16)
            def act_transposed(t):
                act.wait_ge(xn_t_psum, t + 1)
                nc.scalar.copy(xn_t[:, :, t * P:(t + 1) * P],
                               bank[t % 2][:, 0:KD * P].rearrange("p (k c) -> p k c", k=KD)).then_inc(xn_t_ready, 1)

            for i in range(2):
                half = slice(i * HALF, (i + 1) * HALF)
                act.wait_ge(var_ready, i + 1)
                nc.scalar.activation(std[:, half], stat[:, 9, half], ACT.Sqrt).then_inc(std_ready, 1)
                act.wait_ge(shift_ready, i + 1)
                for t in range(i * HALF + 1, (i + 1) * HALF, 2):
                    nc.scalar.activation(xn[:, t, :], x_sb[:, t, :], ACT.Identity, bias=shift[:, t:t + 1],
                                         scale=rstd[:, t:t + 1]).then_inc(xn_ready[1], 1)
                for t in range(i * HALF, (i + 1) * HALF):
                    act_transposed(t)
            act.wait_ge(small_loaded, 48)
            nc.scalar.activation(a_exp[:, :], a_log, ACT.Exp).then_inc(exp_out_ready, 1)
            act.wait_ge(exp_in_ready, 1)
            nc.scalar.activation(ex[:, :, :], lg[:, :, :], ACT.Exp).then_inc(exp_out_ready, 1)
            act.wait_ge(exp_in_ready, 2)
            nc.scalar.activation(dtw[:, 2, :, :], dtw[:, 1, :, :], ACT.Exp).then_inc(exp_out_ready, 1)

            def act_squares(e, pair, u, first=False):
                act.wait_ge(w_loaded[0][u], (pair + 1) * 16)
                if not first:
                    act.wait_ge(squares_psum, e)
                nc.scalar.activation(w_part(0, u, 0), w_whole(0, u), ACT.Square, accum_out=squares[:, 0:1]
                                     ).then_inc(squares_ready, 1)

            def act_squares2(e, pair, u):
                act.wait_ge(bias_loaded[u], (pair + 1) * 32)
                nc.scalar.activation(nothing[:, 0:FT], b1[:, u, :], ACT.Square, accum_out=squares[:, 2:3]
                                     ).then_inc(squares_ready, 1)
                act.wait_ge(w_loaded[1][u], (pair + 1) * 16)
                nc.scalar.activation(w_part(0, u, 1)[:, 0:FS * DM], w_whole(1, u), ACT.Square,
                                     accum_out=squares[:, 1:2]).then_inc(squares_ready, 1)

            def act_high(j, e, u):
                act.wait_ge(scale_ready, e + 1)
                act.wait_ge(squares_ready, e * 3 + 1)
                nc.scalar.activation(w_part(j, u, 0), w_whole(j, u), ACT.Copy, scale=scale(u, f"w{j + 1}")
                                     ).then_inc(w_high[j], 1)

            def conv_silu(j):
                _, m, n = XBC[j]
                act.wait_ge(conv_ready, j + 1)
                dst = bc[:, n * SPAN:(n + 1) * SPAN] if m == HT else xc[:, m, n * SPAN:(n + 1) * SPAN]
                nc.scalar.activation(dst, conv[:, j % 4, :], ACT.Silu, bias=conv_bias(m)).then_inc(conv_read, 1)
                if m == HT:
                    act.wait_ge(conv_read, j + 1)
                    act.dma_start(c_low[:, n * SPAN:(n + 1) * SPAN], bc[STATE:2 * STATE, n * SPAN:(n + 1) * SPAN]
                                  ).then_inc(c_moved[n], 16)

            act_squares(0, 0, 0, first=True)
            j = 0
            for i, (kind, m, n) in enumerate(PROJ):
                if i == 2:
                    act_high(0, 0, 0)
                if i == SQUARES_AT:
                    act_squares(1, 0, 1)
                    act_squares2(1, 0, 1)
                if i == PLACES_AT + 4:
                    act.wait_ge(decay_psum, 1)
                    nc.scalar.activation(decay[:, :, :], bank[2][:, 0:TILES * HEADS].rearrange("p (t h) -> p t h", h=HEADS),
                                         ACT.Exp).then_inc(decay_ready, 1)
                src = bank[PROJ_BANKS[i % NPB]]
                if kind == "z":
                    act.wait_ge(proj_psum, i + 1)
                    nc.scalar.activation(zs[:, m, n * SPAN:(n + 1) * SPAN], src[:, :], ACT.Silu).then_inc(z_ready, 1)
                else:
                    if j >= 4:
                        conv_silu(j - 4)
                        act.wait_ge(conv_read, j - 3)
                    act.wait_ge(proj_psum, i + 1)
                    nc.scalar.activation(conv[:, j % 4, :], src[:, :], ACT.Copy, scale=tap(m, TAPS - 1)
                                         ).then_inc(tap_ready, 1)
                    j += 1
            for j in range(len(XBC) - 4, len(XBC)):
                conv_silu(j)

            def gelu_table():
                nc.scalar.activation(nothing[:, FT:FT + 1], zeros[:, 0:1], ACT.Gelu)

            gelu_table()

            def act_step(n, pair, u, first=False, last=False):
                if not first and not last:
                    act_squares(n + 1, pair + u, 1 - u)
                act.wait_ge(bias_loaded[u], (pair + 1) * 32)
                for f in range(FT):
                    act.wait_ge(fc1_psum, n * FT + f + 1)
                    nc.scalar.activation(hid[:, f, :], bank[FC1_BANKS[f % NB1]][:, 0:CAP], ACT.Gelu,
                                         bias=b1[:, u, f:f + 1], scale=scale(u, "fc1_back")).then_inc(hid_ready, 1)
                    if f == 2 and not first:
                        act_square(n - 1)
                if not first and not last:
                    act_squares2(n + 1, pair + u, 1 - u)
                if not first:
                    act_store(n - 1)
                act.wait_ge(seg_psum, n + 1)
                nc.scalar.activation(mix[:, :, :], bank[SEG][:, :].rearrange("p (h l) -> p h l", h=HEADS),
                                     ACT.Exp).then_inc(seg_ready, 1)
                act.wait_ge(last_in_psum, n + 1)
                low = bank[OUT_THEN_STATE][0:STATE, :].rearrange("p (h l) -> p h l", h=HEADS)
                if first:
                    for q in scattered:
                        act.wait_ge(q, 16 * CHOICES * TILES // 4)
                if u == 0:
                    nc.scalar.copy(b_tok[:, :], bank[OUT_THEN_STATE][:, 0:STATE]).then_inc(b_tok_ready, 1)
                    act_high(0, n + 1, 1 - u)
                    act_high(1, n + 1, 1 - u)
                    gelu_table()
                    act.wait_ge(state_psum, pair + 1)
                    nc.scalar.copy(state[:, :, :], low).then_inc(state_ready, 1)
                else:
                    nc.scalar.activation(c_dec[:, :, :], low, ACT.Exp).then_inc(cexp_ready, 1)
                    if not last:
                        act_high(0, n + 1, 1 - u)
                        act_high(1, n + 1, 1 - u)
                        gelu_table()

            def act_square(n):
                act.wait_ge(g_ready, n + 1)
                nc.scalar.square(gsq[:, :, :], g[:, :, :]).then_inc(gsq_ready, 1)

            def act_store(n):
                act.wait_ge(s_psum, n + 1)
                nc.scalar.copy(s_out[:, bass.ds(n, 1), :].rearrange("p a c -> p (a c)"),
                               bank[OUT_THEN_STATE][:, 0:DM + 1]).then_inc(s_ready, 1)

            act_step(0, 0, 0, first=True)
            with act.Fori(0, STEPS // 2 - 1) as i:
                act_step(i * 2 + 1, i, 1)
                act_step(i * 2 + 2, i + 1, 0)
            act_step(STEPS - 1, STEPS // 2 - 1, 1, last=True)
            nc.scalar.activation(nothing[:, FT:FT + 1], zeros[:, 0:1], ACT.Silu)
            act_square(STEPS - 1)
            act_store(STEPS - 1)

            for i in range(4):
                t = slice(2 * i, 2 * i + 2)
                act.wait_ge(moe_loaded[i], 16)
                nc.scalar.activation(moe[:, 1, t, :], moe[:, 0, t, :], ACT.Silu).then_inc(moe_silu, 1)

        @block.vector
        def _(dve):
            chained = [0]

            def link(ins):
                chained[0] += 1
                ins.then_inc(dve_steps, 1)
                dve.wait_ge(dve_steps, chained[0])

            def step(ins):
                chained[0] += 1
                ins.then_inc(dve_steps, 1)

            V = nc.vector

            def stats(i):
                dve.wait_ge(x_loaded[i], 16)
                for t in range(i * HALF, (i + 1) * HALF):
                    step(V.bn_stats(bn[:, t, :], x_sb[:, t, :]))
                dve.wait_ge(dve_steps, chained[0])
                for t in range(i * HALF, (i + 1) * HALF):
                    step(V.bn_aggr(mv[:, t, :], bn[:, t, :]))
                dve.wait_ge(dve_steps, chained[0])
                half = slice(i * HALF, (i + 1) * HALF)
                V.tensor_scalar(stat[:, 9, half], mv[:, half, 1], EPS, None, ALU.add).then_inc(var_ready, 1)

            def normalise(i):
                half = slice(i * HALF, (i + 1) * HALF)
                dve.wait_ge(std_ready, i + 1)
                link(V.reciprocal(rstd[:, half], std[:, half]))
                V.scalar_tensor_tensor(shift[:, half], mv[:, half, 0], -1.0, rstd[:, half], ALU.mult, ALU.mult
                                       ).then_inc(shift_ready, 1)
                for t in range(i * HALF, (i + 1) * HALF, 2):
                    V.tensor_scalar(xn[:, t, :], x_sb[:, t, :], mv[:, t, 0:1], rstd[:, t:t + 1],
                                    ALU.subtract, ALU.mult).then_inc(xn_ready[0], 1)

            def low_parts(tiles):
                for t in tiles:
                    dve.wait_ge(high_ready, t + 1)
                    V.scalar_tensor_tensor(halves[t][1], xn[:, t, :], XN_SCALE, halves[t][0], ALU.mult, ALU.subtract
                                           ).then_inc(low_ready, 1)

            def power(to, exponents, slope, at_zero):
                return V.tensor_scalar(to.bitcast(I32), exponents.bitcast(I32), slope * EXP1,
                                       float(127 + at_zero) * EXP1, ALU.mult, ALU.add)

            def dve_scale(e, u, sums, first=False):
                dve.wait_ge(squares_psum, e + 1)
                if first:
                    V.tensor_scalar(scale(u, "sums"), sums, 2.0 ** -43, None, ALU.max).then_inc(sums_ready, 1)
                    dve.wait_ge(sums_ready, 1)
                else:
                    V.tensor_scalar(scale(u, "sum2"), sums[:, 1:2], 2.0 ** -43, None, ALU.max).then_inc(sums_ready, 1)
                    V.tensor_scalar(scale(u, "bias_sum"), sums[:, 2:3], 2.0 ** -43, None, ALU.max
                                    ).then_inc(sums_ready, 1)
                    dve.wait_ge(sums_ready, e * 3)
                    V.tensor_tensor(scale(u, "sums"), sums[:, 0:1], scale(u, "bias_sum"), ALU.add
                                    ).then_inc(sums_ready, 1)
                    dve.wait_ge(sums_ready, e * 3 + 1)
                n = 1 if first else 2
                V.tensor_scalar(scale(u, "exponents", n).bitcast(U32), scale(u, "sums", n).bitcast(U32), 24, None,
                                ALU.logical_shift_right).then_inc(exponent_ready, 1)
                dve.wait_ge(exponent_ready, e + 1)
                power(scale(u, "w1", n), scale(u, "exponents", n), -1.0, 77).then_inc(scale_ready, 1)
                power(scale(u, "fc1_back"), scale(u, "exponents"), 1.0, -77 - 10).then_inc(backs_ready, 1)
                if not first:
                    power(scale(u, "hidden"), scale(u, "exponents"), -1.0, 77 - 5).then_inc(backs_ready, 1)
                    power(scale(u, "hidden_back"), scale(u, "exponents"), 1.0, 5 - 77).then_inc(backs_ready, 1)
                    power(scale(u, "w2_back"), scale(u, "exponent2"), 1.0, -77).then_inc(backs_ready, 1)

            def dve_fc2_scales(e, u):
                dve.wait_ge(scale_ready, e + 1)
                dve.wait_ge(backs_ready, e * 4 + 1)
                V.tensor_tensor(scale(u, "hidden_w2"), scale(u, "hidden"), scale(u, "w2"), ALU.mult
                                ).then_inc(fc2_scales_ready, 1)
                V.tensor_tensor(scale(u, "fc2_back"), scale(u, "hidden_back"), scale(u, "w2_back"), ALU.mult
                                ).then_inc(fc2_scales_ready, 1)

            def dve_low(j, e, u):
                dve.wait_ge(scale_ready, e + 1)
                dve.wait_ge(w_high[j], e + 1 - j)
                V.scalar_tensor_tensor(w_part(j, u, 1), w_whole(j, u), scale(u, f"w{j + 1}"), w_part(j, u, 0),
                                       ALU.mult, ALU.subtract).then_inc(w_split[j], 1)

            def dve_hidden(n, u, f):
                dve.wait_ge(hid_ready, NB1 + n * FT + f + 2)
                two = hid[:, f:f + 2, :]
                if f < FS:
                    high, low = hids[:, 0, f:f + 2, :], hids[:, 1, f:f + 2, :]
                    V.tensor_scalar(high, two, scale(u, "hidden"), None, ALU.mult).then_inc(hid_high, 1)
                    dve.wait_ge(hid_high, (n - 1) * (FS // 2) + f // 2 + 1)
                    V.scalar_tensor_tensor(low, two, scale(u, "hidden"), high, ALU.mult, ALU.subtract
                                           ).then_inc(hid_split, 1)
                else:
                    V.tensor_scalar(two, two, scale(u, "hidden_w2"), None, ALU.mult).then_inc(hid_split, 1)

            stats(0)
            normalise(0)
            stats(1)
            normalise(1)
            low_parts(range(HALF))

            def over_e(a):
                return a.unsqueeze(2).to_broadcast([P, a.shape[1], EXPERTS])

            small = bank[3][:, 0:TILES * NSMALL].rearrange("p (t c) -> p t c", c=NSMALL)
            logits = small[:, :, HEADS:NSMALL]
            scores = [sc[:, k, :, :] for k in range(CHOICES)]
            hots = [hot[:, k * TILES:(k + 1) * TILES, :] for k in range(CHOICES)]
            top = [stat[:, 3 + k, :] for k in range(CHOICES)]
            preferred = prefer[:, :].unsqueeze(1).to_broadcast([P, TILES, EXPERTS])
            e_, d_, z_, z2, p_ = (dtw[:, n, :, :] for n in (2, 3, 4, 5, 6))
            dve.wait_ge(small_psum, 1)
            dve.wait_ge(small_loaded, 48)
            dve.wait_ge(masks_ready, 11)
            r_count, d_count = [0], [0]

            def r(ins):
                r_count[0] += 1
                ins.then_inc(router_steps, 1)

            def d(ins):
                d_count[0] += 1
                ins.then_inc(dt_steps, 1)

            def after_r():
                dve.wait_ge(router_steps, r_count[0])

            def after_d():
                dve.wait_ge(dt_steps, d_count[0])

            r(V.tensor_reduce(stat[:, 0, :], logits, AX_X, ALU.max))
            d(V.tensor_tensor(dtw[:, 0, :, :], small[:, :, 0:HEADS],
                              dt_bias.unsqueeze(1).to_broadcast([P, TILES, HEADS]), ALU.add))
            after_r()
            V.tensor_tensor(lg[:, :, :], logits, over_e(stat[:, 0, :]), ALU.subtract).then_inc(exp_in_ready, 1)
            after_d()
            V.scalar_tensor_tensor(dtw[:, 1, :, :], dtw[:, 0, :, :], -1.0, dtw[:, 0, :, :],
                                   ALU.mult, ALU.min).then_inc(exp_in_ready, 1)
            d(V.tensor_scalar(dtw[:, 7, :, :], dtw[:, 0, :, :], 0.0, None, ALU.max))
            dve.wait_ge(exp_out_ready, 2)
            r(V.tensor_reduce(stat[:, 1, :], ex[:, :, :], AX_X, ALU.add))
            dve.wait_ge(exp_out_ready, 3)
            d(V.tensor_scalar(d_, e_, 2.0, None, ALU.add))
            after_r()
            r(V.reciprocal(stat[:, 2, :], stat[:, 1, :]))
            after_d()
            d(V.reciprocal(d_, d_))
            after_r()
            r(V.tensor_tensor(scores[0], ex[:, :, :], over_e(stat[:, 2, :]), ALU.mult))
            after_d()
            d(V.tensor_tensor(z_, e_, d_, ALU.mult))
            after_r()
            r(V.tensor_reduce(top[0], scores[0], AX_X, ALU.max))
            after_d()
            d(V.tensor_tensor(z2, z_, z_, ALU.mult))
            after_r()
            r(V.tensor_tensor(key[:, :, :], scores[0], over_e(top[0]), ALU.is_equal))
            after_d()
            d(V.tensor_scalar(p_, z2, 1.0 / 17, None, ALU.mult))
            after_r()
            r(V.tensor_tensor(key[:, :, :], key[:, :, :], preferred, ALU.mult))
            after_d()
            d(V.scalar_tensor_tensor(p_, p_, 1.0 / 15, z2, ALU.add, ALU.mult))
            after_r()
            r(V.tensor_reduce(stat[:, 5, :], key[:, :, :], AX_X, ALU.max))
            after_d()
            d(V.scalar_tensor_tensor(p_, p_, 1.0 / 13, z2, ALU.add, ALU.mult))
            after_r()
            r(V.tensor_tensor(hots[0], key[:, :, :], over_e(stat[:, 5, :]), ALU.is_equal))
            after_d()
            d(V.scalar_tensor_tensor(p_, p_, 1.0 / 11, z2, ALU.add, ALU.mult))
            after_r()
            r(V.scalar_tensor_tensor(scores[1], hots[0], -2.0, scores[0], ALU.mult, ALU.add))
            after_d()
            d(V.scalar_tensor_tensor(p_, p_, 1.0 / 9, z2, ALU.add, ALU.mult))
            after_r()
            r(V.tensor_reduce(top[1], scores[1], AX_X, ALU.max))
            after_d()
            d(V.scalar_tensor_tensor(p_, p_, 1.0 / 7, z2, ALU.add, ALU.mult))
            after_r()
            r(V.tensor_tensor(key[:, :, :], scores[1], over_e(top[1]), ALU.is_equal))
            after_d()
            d(V.scalar_tensor_tensor(p_, p_, 1.0 / 5, z2, ALU.add, ALU.mult))
            after_r()
            r(V.tensor_tensor(key[:, :, :], key[:, :, :], preferred, ALU.mult))
            after_d()
            d(V.scalar_tensor_tensor(p_, p_, 1.0 / 3, z2, ALU.add, ALU.mult))
            after_r()
            r(V.tensor_reduce(stat[:, 5, :], key[:, :, :], AX_X, ALU.max))
            after_d()
            d(V.scalar_tensor_tensor(p_, p_, 1.0, z_, ALU.add, ALU.mult))
            after_r()
            V.tensor_tensor(hots[1], key[:, :, :], over_e(stat[:, 5, :]), ALU.is_equal).then_inc(hot_ready, 1)
            after_d()
            d(V.scalar_tensor_tensor(dt_sb[:, :, :], p_, 2.0, dtw[:, 7, :, :], ALU.mult, ALU.add))
            r(V.tensor_tensor(stat[:, 6, :], top[0], top[1], ALU.add))
            after_d()
            V.scalar_tensor_tensor(a_dt[:, :, :], dt_sb[:, :, :], -1.0,
                                   a_exp[:, :].unsqueeze(1).to_broadcast([P, TILES, HEADS]),
                                   ALU.mult, ALU.mult).then_inc(a_dt_ready, 1)
            after_r()
            r(V.tensor_scalar(stat[:, 6, :], stat[:, 6, :], 1e-9, None, ALU.max))
            after_r()
            r(V.reciprocal(stat[:, 7, :], stat[:, 6, :]))
            after_r()
            for k in range(CHOICES):
                V.tensor_tensor(rec[:, k, :, DM], top[k], stat[:, 7, :], ALU.mult).then_inc(gates_ready, 1)

            low_parts(range(HALF, TILES))
            dve_scale(0, 0, FIRST_SUM, first=True)
            dve.wait_ge(place_psum, 1)
            places = bank[2][:, 0:P].rearrange("p (q e) -> p q e", e=EXPERTS)
            link(V.tensor_scalar(place[:, 0, :, :], places, float(CAP), DROPPED, ALU.is_ge, ALU.mult))
            link(V.tensor_tensor(place[:, 1, :, :], places, place[:, 0, :, :], ALU.add))
            link(V.tensor_tensor(place[:, 2, :, :], place[:, 1, :, :], slot0[:, :, :], ALU.add))
            link(V.tensor_tensor(place[:, 0, :, :], place[:, 2, :, :], hot[:, :, :], ALU.mult))
            link(V.tensor_reduce(slot_f[:, :], place[:, 0, :, :], AX_X, ALU.add))
            V.tensor_copy(slot_i[:, :], slot_f[:, :]).then_inc(slots_known, 1)

            def dve_slots(e, pair, u):
                dve.wait_ge(slots_t_psum, e + 1)
                V.tensor_copy(slots_t[:, u, :, :, :].rearrange("p a k s -> p (a k s)"), bank[TRANSPOSED][:, :].bitcast(F16)
                              ).then_inc(slots_t_ready, 1)
                dve.wait_ge(slots_loaded[u], (pair + 1) * 16)
                dve.wait_ge(eo_free, e + 1)
                V.tensor_copy(gate[:, u, :], slots[:, u, :, DM])
                V.tensor_scalar(row_t[:, :], slots[:, u, :, DM + 1], 0.0, DROPPED, ALU.is_equal, ALU.mult
                                ).then_inc(row_step, 1)
                dve.wait_ge(row_step, e + 1)
                V.scalar_tensor_tensor(row_i[:, u, :], slots[:, u, :, DM + 1], -1.0, row_t[:, :],
                                       ALU.add, ALU.add).then_inc(slot_info, 1)

            for j0 in range(0, len(XBC), 2):
                if j0 == 2:
                    dve_low(0, 0, 0)
                if j0 == DECAY_AT:
                    dve.wait_ge(decay_ready, 1)
                    V.tensor_tensor(decay[:, :, :], decay[:, :, :], dt_sb[:, :, :], ALU.mult).then_inc(decay_used, 1)
                for d in range(1, TAPS):
                    if j0 == len(XBC) - 2 and d == TAPS - 1:
                        dve.sem_inc(eo_free, 2)
                        dve_slots(0, 0, 0)
                    for j in (j0, j0 + 1):
                        i, m, n = XBC[j]
                        src = bank[PROJ_BANKS[i % NPB]][:, :].rearrange("p (b l) -> p b l", l=SEQ)
                        acc = conv[:, j % 4, :].rearrange("p (b l) -> p b l", l=SEQ)
                        if d == 1:
                            dve.wait_ge(tap_ready, j + 1)
                        else:
                            dve.wait_ge(conv_steps, 2 * (d - 2) + 2 * j0 + j - j0 + 1)
                        ins = V.scalar_tensor_tensor(acc[:, :, d:], src[:, :, 0:SEQ - d], tap(m, TAPS - 1 - d),
                                                     acc[:, :, d:], ALU.mult, ALU.add)
                        ins.then_inc(conv_steps if d < TAPS - 1 else conv_ready, 1)

            dve.wait_ge(conv_read, len(XBC))
            dve.wait_ge(z_ready, HT * SPANS)

            def dve_step(n, pair, u, first=False, last=False):
                now = bass.ds(n * P, P)
                if not first:
                    dve.wait_ge(fc2_scales_ready, n * 2)
                    dve_hidden(n, u, 0)
                    sum_squares(n - 1)
                    dve_hidden(n, u, 2)
                x_tok = bank[TRANSPOSED][:, :].rearrange("p (h l) -> p h l", h=HEADS)

                def per_step(a):
                    return a[:, bass.ds(n, 1), :].rearrange("p a h -> p (a h)").unsqueeze(2).to_broadcast([P, HEADS, P])

                dve.wait_ge(cb_psum, n + 1)
                V.tensor_tensor(cb[:, :], bank[CB_THEN_Y][:, 0:P], upto[:, :], ALU.mult).then_inc(cb_ready, 1)
                dve.wait_ge(xt_psum, n + 1)
                V.tensor_tensor(xs[:, :, :], x_tok, per_step(dt_sb), ALU.mult).then_inc(xs_ready, 1)
                if u == 0:
                    V.tensor_tensor(xd[:, :, :], x_tok, per_step(decay), ALU.mult).then_inc(xd_ready, 1)
                if not first:
                    for f in range(4, FT, 2):
                        dve_hidden(n, u, f)
                if not last:
                    dve_scale(n + 1, 1 - u, bank[CB_THEN_Y][:, P:P + 3])
                dve.wait_ge(cb_ready, n + 1)
                dve.wait_ge(seg_ready, n + 1)
                V.tensor_tensor(mix[:, :, :], mix[:, :, :], cb[:, :].unsqueeze(1).to_broadcast([P, HEADS, P]),
                                ALU.mult).then_inc(mix_ready, 1)
                if u == 1:
                    dve.wait_ge(cexp_ready, pair + 1)
                    V.tensor_tensor(c_dec[:, :, :], c_dec[:, :, :],
                                    c_low[:, now].unsqueeze(1).to_broadcast([STATE, HEADS, P]), ALU.mult
                                    ).then_inc(cdec_ready, 1)
                if not last:
                    dve_slots(n + 1, pair + u, 1 - u)
                    dve_low(0, n + 1, 1 - u)
                if last:
                    normalise_rows(0, STEPS - 1)
                for h in range(CH):
                    dve.wait_ge(fc2_psum, n * CH + h + 1)
                    if first:
                        V.tensor_tensor(eo[:, u, h, :], bank[FC2_BANKS[h]][:, 0:DM], b2[:, u, :], ALU.add
                                        ).then_inc(fc2_read, 1)
                    else:
                        V.scalar_tensor_tensor(eo[:, u, h, :], bank[FC2_BANKS[h]][:, 0:DM], scale(u, "fc2_back"),
                                               b2[:, u, :], ALU.mult, ALU.add).then_inc(fc2_read, 1)
                    dve.wait_ge(fc2_read, CH + n * CH + h + 1)
                    V.tensor_scalar(eo[:, u, h, :], eo[:, u, h, :], gate[:, u, h:h + 1], None, ALU.mult
                                    ).then_inc(eo_ready, 1)
                dve_gated(n, now)
                if not last:
                    dve_low(1, n + 1, 1 - u)
                    dve_fc2_scales(n + 1, 1 - u)

            def normalise_rows(first, end, work={}):
                dve.wait_ge(s_ready, end)
                ms, y_, t_ = (rms[:, k, first:end] for k in range(3))
                count = [0]

                def newton(ins):
                    step(ins)
                    if count[0] in work:
                        multiply(work[count[0]])
                    count[0] += 1
                    dve.wait_ge(dve_steps, chained[0])

                newton(V.tensor_scalar(ms, s_out[:, first:end, DM], 1.0 / DI, EPS, ALU.mult, ALU.add))
                newton(V.tensor_scalar(y_.bitcast(U32), ms.bitcast(U32), 1, None, ALU.logical_shift_right))
                newton(V.tensor_scalar(y_.bitcast(I32), y_.bitcast(I32), -1.0, float(0x5F3759DF), ALU.mult, ALU.add))
                for _ in range(3):
                    newton(V.tensor_tensor(t_, y_, y_, ALU.mult))
                    newton(V.scalar_tensor_tensor(t_, t_, -0.5, ms, ALU.mult, ALU.mult))
                    newton(V.scalar_tensor_tensor(y_, t_, 1.5, y_, ALU.add, ALU.mult))
                for t in range(first, end):
                    step(V.tensor_scalar(s_out[:, t, 0:DM], s_out[:, t, 0:DM], rms[:, 1, t:t + 1], None, ALU.mult))

            def dve_gated(n, now):
                dve.wait_ge(y_psum, n + 1)
                for h in range(HT):
                    V.scalar_tensor_tensor(g[:, h, :], xc[:, h, now], d_skip(h), bank[CB_THEN_Y][:, h * P:(h + 1) * P],
                                           ALU.mult, ALU.add).then_inc(y_read, 1)
                dve.wait_ge(y_read, n * HT + HT)
                V.tensor_tensor(g[:, :, :], g[:, :, :], zs[:, :, now], ALU.mult).then_inc(g_ready, 1)

            def sum_squares(n):
                dve.wait_ge(gsq_ready, n + 1)
                V.tensor_reduce(gsum[:, :], gsq[:, :, :].rearrange("p h l -> p l h"), AX_X, ALU.add
                                ).then_inc(gsum_ready, 1)

            dve.wait_ge(bias_loaded[0], 32)
            dve.wait_ge(bias_loaded[1], 32)
            dve_step(0, 0, 0, first=True)
            with dve.Fori(0, STEPS // 2 - 1) as i:
                for u in (1, 0):
                    dve.wait_ge(bias_loaded[u], (i + 2 - u) * 32)
                    dve_step(i * 2 + 2 - u, i + 1 - u, u)
            dve.wait_ge(bias_loaded[1], STEPS // 2 * 32)
            dve_step(STEPS - 1, STEPS // 2 - 1, 1, last=True)
            sum_squares(STEPS - 1)

            def multiply(i):
                t = slice(2 * i, 2 * i + 2)
                dve.wait_ge(moe_silu, i + 1)
                V.tensor_tensor(moe[:, 0, t, :], s_out[:, t, 0:DM], moe[:, 1, t, :], ALU.mult).then_inc(product_ready, 1)

            normalise_rows(STEPS - 1, STEPS, work={2: 0, 5: 1, 8: 2})
            dve.wait_ge(dve_steps, chained[0])
            multiply(3)
            dve.wait_ge(product_ready, 4)
            V.tensor_tensor(moe[:, 0, 6:8, :], moe[:, 0, 6:8, :], x_sb[:, 6:8, :], ALU.add).then_inc(out_ready[1], 1)

        @block.tensor
        def _(pe):
            T = nc.tensor

            pe.wait_ge(zeros_ready, 1)
            for _ in range(WARM_UP):
                T.matmul(bank[7][:, 0:P], zeros[:, 0:P], zeros[:, 0:P], start=True, stop=True)

            pe.wait_ge(masks_ready, 11)
            pe.wait_ge(small_loaded, 48)

            def small_products(t):
                pe.wait_ge(xn_t_ready, t + 1)
                for k in range(KD):
                    last = T.matmul(bank[3][:, t * NSMALL:(t + 1) * NSMALL], xn_t[:, k, t * P:(t + 1) * P],
                                    wsmall[:, k, :], start=(k == 0), stop=(k == KD - 1))
                return last

            for t in range(TILES):
                pe.wait_ge(xn_ready[t % 2], t // 2 + 1)
                if t >= 2:
                    pe.wait_ge(xn_t_ready, t - 1)
                for k in range(KD):
                    last = T.transpose(bank[t % 2][:, k * P:(k + 1) * P], xn[:, t, k * P:(k + 1) * P], ident[:, :])
                last.then_inc(xn_t_psum, 1)
                if t >= 2:
                    small_products(t - 2)
            small_products(TILES - 2)
            small_products(TILES - 1).then_inc(small_psum, 1)

            def place_products():
                pe.wait_ge(hot_ready, 1)
                q = CHOICES * TILES
                rows = hot[:, :, :]
                T.matmul(bank[2][:, 0:q * EXPERTS], before16[:, :], rows.rearrange("p q e -> p (q e)"),
                         start=True, stop=False)
                for n in range(q - 1):
                    dst = bank[2][:, (n + 1) * EXPERTS:q * EXPERTS].rearrange("p (q e) -> p q e", e=EXPERTS)
                    last = T.matmul(dst, ones16[:, :],
                                    hot[:, n, :].unsqueeze(1).to_broadcast([P, q - 1 - n, EXPERTS]),
                                    start=False, stop=(n == q - 2))
                last.then_inc(place_psum, 1)

            def slots_transposed(e, pair, u):
                pe.wait_ge(slots_loaded[u], (pair + 1) * 16)
                for h in range(CH):
                    rows = slots[:, u, h, 0:DM].bitcast(F16)
                    for k in range(PARTS * KD):
                        last = T.transpose(bank[TRANSPOSED][:, :].bitcast(F16)[:, k * CAP + h * P:k * CAP + (h + 1) * P],
                                           rows[:, k * P:(k + 1) * P], ident16[:, :])
                last.then_inc(slots_t_psum, 1)

            def weight_squares(e, sums):
                pe.wait_ge(squares_ready, e * 3 + 1)
                T.matmul(sums, ones[:, :], squares[:, 0:sums.shape[1]], start=True, stop=True).then_inc(squares_psum, 1)

            def projected_read(i):
                kind, m, n = PROJ[i]
                if kind == "z":
                    pe.wait_ge(z_ready, Z.index((kind, m, n)) + 1)
                else:
                    pe.wait_ge(conv_ready, convolved(m, n))

            for i, (kind, m, n) in enumerate(PROJ):
                pe.wait_ge(win_loaded[0 if kind == "z" else 1], 16)
                if i == 2:
                    pe.wait_ge(exp_in_ready, 2)
                    weight_squares(0, FIRST_SUM)
                if i == PLACES_AT:
                    place_products()
                if i == PLACES_AT + 4:
                    pe.wait_ge(a_dt_ready, 1)
                    pe.wait_ge(slots_known, 1)
                    T.matmul(bank[2][:, 0:TILES * HEADS], later[:, :], a_dt[:, :, :].rearrange("p t h -> p (t h)"),
                             start=True, stop=True).then_inc(decay_psum, 1)
                if i == 1:
                    pe.wait_ge(xn_t_ready, TILES)
                if i >= NPB:
                    projected_read(i - NPB)
                c = col0(kind, m)
                for k in range(KD):
                    last = T.matmul(bank[PROJ_BANKS[i % NPB]][:, :], win[:, k, c:c + P], xn_t[:, k, n * SPAN:(n + 1) * SPAN],
                                    start=(k == 0), stop=(k == KD - 1))
                last.then_inc(proj_psum, 1)

            def fc1(n, pair, u, tiles=range(FT)):
                pe.wait_ge(slots_t_ready, n + 1)
                pe.wait_ge(w_split[0], n + 1)
                for f in tiles:
                    pe.wait_ge(hid_ready, n * FT + f + 1)
                    if FC1_BANKS[f % NB1] in FC2_BANKS:
                        pe.wait_ge(fc2_read, n * CH + 1 + FC2_BANKS.index(FC1_BANKS[f % NB1]))
                    for k in range(KD):
                        for a, b in PRODUCTS:
                            last = T.matmul(bank[FC1_BANKS[f % NB1]][:, 0:CAP], w1s[:, u, a, k, f * P:(f + 1) * P],
                                            slots_t[:, u, b, k, :], start=(k == 0 and (a, b) == PRODUCTS[0]),
                                            stop=(k == KD - 1 and (a, b) == PRODUCTS[-1]))
                    last.then_inc(fc1_psum, 1)

            def fc2(n, u, h, first):
                if first:
                    pe.wait_ge(hid_ready, NB1 + FT)
                else:
                    pe.wait_ge(hid_split, n * (FT // 2))
                pe.wait_ge(fc2_read, n * CH + h + 1)
                for f in range(FT):
                    dst, tokens = bank[FC2_BANKS[h]][:, 0:DM], slice(h * P, (h + 1) * P)
                    split = f < FS and not first
                    for a, b in PRODUCTS if split else [(0, 0)]:
                        rows, weights = ((hids[:, a, f, tokens], w2s[:, u, b, f, :]) if split else
                                         (hid[:, f, tokens], w2[:, u, f, :]))
                        last = T.matmul(dst, rows, weights, start=(f == 0 and a == b), stop=(f == FT - 1 and a >= b))
                last.then_inc(fc2_psum, 1)

            def out_proj(n):
                dst = bank[OUT_THEN_STATE]
                pe.wait_ge(g_ready, n + 1)
                for h in range(HT):
                    T.matmul(dst[:, 0:DM], g[:, h, :], wout[:, h, :], start=(h == 0), stop=(h == HT - 1))
                pe.wait_ge(gsum_ready, n + 1)
                T.matmul(dst[:, DM:DM + 1], gsum[:, :], ones[:, 0:1], start=True, stop=True).then_inc(s_psum, 1)

            def chunk_channels(n, pair, u, first):
                now = bass.ds(n * P, P)
                pe.wait_ge(chunk_staged, n * 2 + 2)
                pe.wait_ge(slots_t_ready, n + 1)
                for h in range(HT):
                    last = T.transpose(bank[TRANSPOSED][:, h * P:(h + 1) * P], x_chunk[:, h, :], ident[:, :])
                last.then_inc(xt_psum, 1)
                if not first:
                    pe.wait_ge(y_read, n * HT)
                T.matmul(bank[CB_THEN_Y][:, 0:P], bc_chunk[0:STATE, :], c_low[:, now],
                         start=True, stop=True).then_inc(cb_psum, 1)

            def chunk_decays(n, pair, u, first):
                pe.wait_ge(a_upto_ready, n * 3 + 3)
                if not first:
                    pe.wait_ge(seg_ready, n)
                parts = [a_upto[:, k, :, :].rearrange("p h l -> p (h l)") for k in range(3)]
                for k in range(3):
                    last = T.matmul(bank[SEG][:, :], later16[:, :], parts[k], start=(k == 0), stop=(k == 2))
                last.then_inc(seg_psum, 1)
                if not first:
                    pe.wait_ge(s_ready, n)
                if u == 0:
                    T.transpose(bank[OUT_THEN_STATE][:, 0:P], bc_chunk[:, :], ident[:, :]).then_inc(last_in_psum, 1)
                else:
                    for k in range(3):
                        last = T.matmul(bank[OUT_THEN_STATE][0:STATE, :], ones16[:, 0:STATE], parts[k],
                                        start=(k == 0), stop=(k == 2))
                    last.then_inc(last_in_psum, 1)

            def chunk_state(pair):
                pe.wait_ge(xd_ready, pair + 1)
                pe.wait_ge(b_tok_ready, pair + 1)
                T.matmul(bank[OUT_THEN_STATE][0:STATE, :], b_tok[:, :], xd[:, :, :].rearrange("p h l -> p (h l)"),
                         start=True, stop=True).then_inc(state_psum, 1)

            def chunk_y(n, pair, u, last):
                pe.wait_ge(xs_ready, n + 1)
                pe.wait_ge(mix_ready, n + 1)
                if not last:
                    pe.wait_ge(sums_ready, n * 3 + 4)
                if u == 1:
                    pe.wait_ge(state_ready, pair + 1)
                    pe.wait_ge(cdec_ready, pair + 1)
                for h in range(HEADS):
                    dst = bank[CB_THEN_Y][:, h * P:(h + 1) * P]
                    last = T.matmul(dst, xs[:, h, :], mix[:, h, :], start=True, stop=(u == 0))
                    if u == 1:
                        last = T.matmul(dst, state[:, h, :], c_dec[:, h, :], start=False, stop=True)
                last.then_inc(y_psum, 1)

            def pe_step(n, pair, u, first=False, last=False):
                fc1(n, pair, u, range(NB1) if first else range(FT))
                if first:
                    pe.wait_ge(conv_ready, len(XBC))
                    pe.wait_ge(z_ready, HT * SPANS)
                    for m in range(SPANS):
                        pe.wait_ge(c_moved[m], 16)
                    pe.wait_ge(wout_scaled, HT)
                chunk_channels(n, pair, u, first)
                if not first:
                    out_proj(n - 1)
                if not last:
                    pe.wait_ge(cb_ready, n + 1)
                    weight_squares(n + 1, bank[CB_THEN_Y][:, P:P + 3])
                chunk_decays(n, pair, u, first)
                if first:
                    fc1(n, pair, u, range(NB1, FT))
                pe.wait_ge(xs_ready, n + 1)
                if u == 0:
                    pe.wait_ge(xd_ready, pair + 1)
                if not last:
                    slots_transposed(n + 1, pair + u, 1 - u)
                pe.wait_ge(w_loaded[1][u], (pair + 1) * 16)
                if not first:
                    pe.wait_ge(w_split[1], n)
                fc2(n, u, 0, first)
                if u == 0:
                    chunk_state(pair)
                fc2(n, u, 1, first)
                if u == 1:
                    pe.wait_ge(cexp_ready, pair + 1)
                chunk_y(n, pair, u, last)

            projected_read(len(PROJ) - NPB + PROJ_BANKS.index(TRANSPOSED))
            slots_transposed(0, 0, 0)
            for b in FC1_BANKS:
                if b in PROJ_BANKS:
                    projected_read(len(PROJ) - NPB + PROJ_BANKS.index(b))
            pe.wait_ge(decay_ready, 1)
            pe.wait_ge(sums_ready, 1)
            pe.sem_inc(hid_ready, NB1)
            pe.sem_inc(fc2_read, CH)
            pe_step(0, 0, 0, first=True)
            with pe.Fori(0, STEPS // 2 - 1) as i:
                pe_step(i * 2 + 1, i, 1)
                pe_step(i * 2 + 2, i + 1, 0)
            pe_step(STEPS - 1, STEPS // 2 - 1, 1, last=True)
            out_proj(STEPS - 1)


def kernel(**inputs):
    import numpy as np
    import concourse.bacc as bacc
    from concourse.bass_utils import run_bass_kernel_spmd

    a = {k.split("_", 2)[2]: np.asarray(v) for k, v in inputs.items()}
    di, heads, taps = a["W_out"].shape[1], a["A_log"].shape[0], a["W_conv"].shape[2]
    w_in_t = np.ascontiguousarray(a["W_in"].T)
    small0 = w_in_t.shape[1] - heads
    ctiles = a["W_conv"].shape[0] // P
    channels = np.concatenate([
        a["W_conv"].reshape(ctiles, P, taps).transpose(1, 0, 2).reshape(P, ctiles * taps),
        a["b_conv"].reshape(ctiles, P).T, a["norm_w"].reshape(di // P, P).T], axis=1)
    e, hidden = a["fc1_b"].shape
    arrays = {
        "x": a["u"].reshape(-1, a["u"].shape[-1]),
        "w_in_t": w_in_t,
        "w_small": np.concatenate([w_in_t[:, small0:], a["wg"]], axis=1),
        "head_params": np.concatenate([a["dt_bias"], a["A_log"], a["D"]])[None],
        "channel_params": channels,
        "w_out_t": a["W_out"].T,
        "fc1_w": a["fc1_w"],
        "fc1_b": a["fc1_b"].reshape(e, hidden // P, P).transpose(0, 2, 1),
        "fc2_w": a["fc2_w"],
        "fc2_b": a["fc2_b"],
    }
    arrays = {k: np.ascontiguousarray(v) for k, v in arrays.items()}
    nc = bacc.Bacc("TRN2", target_bir_lowering=False, num_devices=1)
    args = [nc.dram_tensor(k, v.shape, mybir.dt.from_np(v.dtype), kind="ExternalInput").ap() for k, v in arrays.items()]
    args.append(nc.dram_tensor("out", arrays["x"].shape, F32, kind="ExternalOutput").ap())
    layer(nc, *args)
    r = run_bass_kernel_spmd(nc, [arrays], core_ids=[0])
    return r.results[0]["out"].reshape(a["u"].shape)
```
